# Optimizing a Trainium2 kernel written in Bass

```python
import numpy as np
import jax
import jax.numpy as jnp

def _softmax(x, axis=-1):
    return jax.nn.softmax(x, axis=axis)

def _gelu(x):
    return jax.nn.gelu(x, approximate=True)

def _silu(x):
    return jax.nn.silu(x)

def _sigmoid(x):
    return jax.nn.sigmoid(x)

def _layernorm(x, axis=-1, eps=1e-05):
    m = jnp.mean(x, axis=axis, keepdims=True)
    v = jnp.var(x, axis=axis, keepdims=True)
    return (x - m) / jnp.sqrt(v + eps)

def _scatter_add(tgt, idx, src, axis=0):
    return tgt.at[idx].add(src)

def _segment_sum(src, seg, n):
    return jax.ops.segment_sum(src, seg, n)
kernel_name = 'mk_adj_preln_d2_adj_r2_9c2e24'

def setup_inputs(seed: int=0):
    np.random.seed(seed)
    _w = jnp.asarray

    def _rec_inputs():
        import jax
        import jax.numpy as jnp
        _gk = jax.random.key(seed)
        x = -0.0005207 + 1.001 * jax.random.normal(jax.random.fold_in(_gk, 1), (4096, 128), jnp.float32)
        _w = (1.0 + jnp.arange(4096, dtype=jnp.float32)) ** (-0.5)
        _w = _w / _w.mean()
        _pij = jnp.clip(0.00390625 * _w[:, None] * _w[None, :], 0.0, 1.0)
        _a = jax.random.uniform(jax.random.fold_in(_gk, 2), (4096, 4096)) < _pij
        _a = jnp.logical_or(_a, jnp.eye(4096, dtype=bool))
        _af = _a.astype(jnp.float32)
        _af = _af * jax.random.uniform(jax.random.fold_in(_gk, 3), (4096, 4096), jnp.float32, 0.05, 1)
        adj = _af
        return (x, adj)
    x, adj = _rec_inputs()

    def _L0_gnn_setup():
        import jax, jax.numpy as jnp
        import numpy as np
        N = 4096
        D_IN = 128
        D_OUT = 128
        key = jax.random.key(seed)
        k1, k2, k3 = jax.random.split(key, 3)
        input = jax.random.normal(k1, (N, D_IN), dtype=jnp.float32)
        adjacencyMatrix = jax.random.uniform(k2, (N, N), dtype=jnp.float32)
        W = jax.random.normal(k3, (D_OUT, D_IN), dtype=jnp.float32) * (1.0 / np.sqrt(D_IN))
        return {'input': input, 'adjacencyMatrix': adjacencyMatrix, 'W': W}
    _L0_gnn_all = _L0_gnn_setup()
    _L0_gnn_in = {k: v for k, v in _L0_gnn_all.items() if k in ('W',)}
    del _L0_gnn_all

    def _L1_gnn_setup():
        import jax, jax.numpy as jnp
        import numpy as np
        N = 10000
        D = 128
        F = 128
        K = F // 8
        key = jax.random.key(seed)
        k1, k2, k3, k4, k5 = jax.random.split(key, 5)
        h = jax.random.normal(k1, (N, D), dtype=jnp.float32)
        adj = jax.random.uniform(k2, (N, N), dtype=jnp.float32)
        W1 = jax.random.normal(k3, (D, K), dtype=jnp.float32) * 0.05
        W2 = jax.random.normal(k4, (K, D, F), dtype=jnp.float32) * 0.05
        b = jax.random.normal(k5, (K, F), dtype=jnp.float32) * 0.05
        return {'h': h, 'adj': adj, 'W1': W1, 'W2': W2, 'b': b}
    _L1_gnn_all = _L1_gnn_setup()
    _L1_gnn_in = {k: v for k, v in _L1_gnn_all.items() if k in ('W1', 'W2', 'b')}
    del _L1_gnn_all
    return {'x': x, 'adj': adj, 'L0_gnn_W': _L0_gnn_in['W'], 'L1_gnn_W1': _L1_gnn_in['W1'], 'L1_gnn_W2': _L1_gnn_in['W2'], 'L1_gnn_b': _L1_gnn_in['b']}

def reference(x, adj, L0_gnn_W, L1_gnn_W1, L1_gnn_W2, L1_gnn_b):
    import jax
    import jax.numpy as jnp

    def _L0_gnn_ref(input, adjacencyMatrix, W):
        import jax, jax.numpy as jnp
        import numpy as np
        N = 4096
        D_IN = 128
        D_OUT = 128
        d_inv_sqrt = jnp.sum(adjacencyMatrix, axis=1) ** (-0.5)
        A_norm = adjacencyMatrix * d_inv_sqrt[:, None] * d_inv_sqrt[None, :]
        h = A_norm @ input
        return h @ W.T

    def _L1_gnn_ref(h, adj, W1, W2, b):
        import jax, jax.numpy as jnp
        import numpy as np
        N = 10000
        D = 128
        F = 128
        K = F // 8
        node = h @ W1
        hw = jnp.einsum('nc,kcf->nkf', h, W2)
        x = jnp.einsum('nk,nkf->nf', node, hw)
        x = adj @ x
        x = x + node @ b
        return jax.nn.relu(x)
    h = jnp.maximum(_layernorm(x, axis=-1), 0.0)
    x = x + _L0_gnn_ref(h, adj, L0_gnn_W)
    h = jnp.maximum(_layernorm(x, axis=-1), 0.0)
    x = x + _L1_gnn_ref(h, adj, L1_gnn_W1, L1_gnn_W2, L1_gnn_b)
    return x

_drawn_inputs = setup_inputs


def setup_inputs(seed=0):
    import zlib

    import numpy as np

    out = dict(_drawn_inputs(seed))
    spreads = {}
    factors = {}
    for name, (base, spread) in spreads.items():
        noise = np.random.default_rng([zlib.crc32(name.encode()), seed]).standard_normal(out[name].shape)
        drawn = base * np.exp(spread * noise) if base else spread * noise
        out[name] = jnp.asarray(drawn.astype(out[name].dtype))
    for name, factor in factors.items():
        out[name] = (out[name] * factor).astype(out[name].dtype)
    return out
```

```python
from contextlib import ExitStack

import concourse.bass as bass
from concourse import mybir

P = 128
ALU = mybir.AluOpType
ACT = mybir.ActivationFunctionType
F32 = mybir.dt.float32


class Steps:

    def __init__(self, sem, base=0):
        self.sem, self.base, self.n = sem, base, 0

    def inc(self, instruction):
        instruction.then_inc(self.sem, 1)
        self.n += 1

    def wait(self, eng):
        eng.wait_ge(self.sem, self.base + self.n)


def two_graph_layers(nc, x_in, adj, adj_t, w_t, w1, w2, b, out):
    N, F = x_in.shape
    K = w1.shape[1]
    T = N // P
    CH = 512
    NC = N // CH
    G = CH // P
    R = 4
    KQ = CH // F
    Q = K // KQ
    UJ = 4
    NU = T // UJ
    EPS = 1e-5
    assert F == P and NC == 8 and NU == 8 and T % R == 0

    with ExitStack() as ctx:
        def sb(name, shape):
            return ctx.enter_context(nc.sbuf_tensor(name, shape, F32))

        def sem(name):
            return ctx.enter_context(nc.semaphore(name))

        big = sb("big", [P, 2 * NU * UJ * CH])
        ring = [big[:, s * N:(s + 1) * N] for s in range(R)]
        nat = [big[:, (R + s) * N:(R + s + 1) * N] for s in range(2)]
        unit = [big[:, s * UJ * CH:(s + 1) * UJ * CH].rearrange("p (j i) -> p j i", j=UJ) for s in range(2 * NU)]
        xs = sb("xs", [P, N])
        part = sb("part", [P, N])
        mixed = part
        prop_t = sb("prop_t", [P, N])
        node_t = prop_t[0:K, :]
        part_blk = sb("part_blk", [P, 2, P])
        feat = sb("feat", [P, 2, F])
        w2s = sb("w2s", [P, K * F])
        w_ts = sb("w_ts", [P, F])
        w1s = sb("w1s", [P, K])
        bs = sb("bs", [K, F])
        ident = sb("ident", [P, P])
        ones = sb("ones", [P, 2])
        eps = sb("eps", [P, 1])
        zero = sb("zero", [P, 1])
        stats = sb("stats", [P, T, 6])
        tmp = sb("tmp", [P, 5, T])
        ln = sb("ln", [P, T, 2])
        natsum = sb("natsum", [P, T])
        rows = sb("rows", [P, T])
        root = sb("root", [P, T])
        inv = sb("inv", [P, T])
        dnew = sb("dnew", [P, 2])
        deg = sb("deg", [P, T])
        coef = sb("coef", [P, 2, 2])
        prop_g = sb("prop_g", [P, CH])
        ln2 = sb("ln2", [P, G, 2])
        h2 = sb("h2", [P, CH])
        h2t = sb("h2t", [P, 2, CH])
        node = sb("node", [P, 2, G * K])
        mix = sb("mix", [P, 2, F])
        act2 = sb("act2", [P, 2, CH])
        ps = [ctx.enter_context(nc.psum_tensor(f"ps{i}", [P, CH], F32)) for i in range(8)]
        tail, psrow = ps[7], ps[7][:, 0:1]
        ps_y, ps_t, ps_node, ps_node_t = ps[4], ps[5], ps[6], ps[7]

        s_x = sem("x_landed")
        s_w = sem("weights_landed")
        s_nat = [sem(f"nat_landed{i}") for i in range(2)]
        s_ring = [sem(f"strip_landed{i}") for i in range(R)]
        s_unit = [sem(f"unit_landed{i}") for i in range(2 * NU)]
        s_const = sem("constants_set")
        s_natsum = sem("natural_part_summed")
        s_part = sem("part_block_ready")
        s_strip_read = sem("strip_read_by_vector")
        s_tail = sem("tail_product_ready")
        s_tail_added = sem("tail_added")
        s_rowps = sem("rowsum_in_psum")
        s_rows = sem("rowsum_ready")
        s_root = sem("root_ready")
        s_coef = sem("coefficients_ready")
        s_feat = sem("features_ready")
        s_step = sem("step_multiplied")
        s_v = sem("vector_steps")
        s_var = sem("variance_ready")
        s_std = sem("std_ready")
        s_evac = sem("propagated_out_of_psum_by_scalar")
        s_evacv = sem("propagated_out_of_psum_by_vector")
        s_pg = sem("propagated_group_copied")
        s_y = sem("y_ready")
        s_x1 = sem("x1_ready")
        s_passed = sem("scalar_wait_passed")
        s_var2 = sem("variance2_ready")
        s_std2 = sem("std2_ready")
        s_ln2 = sem("ln2_ready")
        s_h2 = sem("h2_ready")
        s_tr = sem("h2_transposed")
        s_h2t = sem("h2t_copied")
        s_nodeps = sem("node_in_psum")
        s_node = sem("node_copied")
        s_node_t = sem("node_t_copied")
        s_prod = sem("mix_products_ready")
        s_prod_read = sem("mix_products_read")
        s_mixed = sem("mixed_ready")
        s_um = sem("unit_multiplied")
        s_relu = sem("chunk_activated")
        s_back = sem("chunk_transposed_back")
        s_res = sem("chunk_result_ready")
        s_out = sem("result_stored")

        block = ctx.enter_context(nc.Block())
        adj_u = adj_t.rearrange("(u j p) i -> u p j i", j=UJ, p=P)

        def tile(buf, t):
            return buf[:, t * P:(t + 1) * P]

        def at(buf, start, size):
            return buf[:, bass.ds(start, size)]

        @block.sync
        def _(sp):
            def load_rows(k):
                if k >= 2:
                    sp.wait_ge(s_natsum, k - 1)
                sp.dma_start(nat[k % 2][:, 0:N - k * P], adj[k * P:(k + 1) * P, k * P:N]).then_inc(s_nat[k % 2], 16)

            load_rows(0)
            sp.dma_start(xs[:, :].rearrange("p (t f) -> p t f", f=F),
                         x_in.rearrange("(t p) f -> p t f", p=P)).then_inc(s_x, 16)
            for k in range(T):
                if k >= R:
                    sp.wait_ge(s_step, k - R + 1)
                    sp.wait_ge(s_strip_read, k - R + 1)
                sp.dma_start(ring[k % R], adj_t[k * P:(k + 1) * P, :]).then_inc(s_ring[k % R], 16)
                if k + 1 < T:
                    load_rows(k + 1)

            def load_unit(c, u, slot):
                sp.dma_start(unit[slot], adj_u[u][:, :, bass.ds(c * CH, CH)]).then_inc(s_unit[slot], 16)

            sp.wait_ge(s_natsum, T)
            for u in range(NU):
                load_unit(1, u, NU + u)
            sp.wait_ge(s_step, T)
            for u in range(NU):
                load_unit(0, u, u)
            with sp.Fori(1, NC // 2) as it:
                for h in range(2):
                    for u in range(NU):
                        sp.wait_ge(s_um, it * (2 * NU) + (h * NU + u + 1 - 2 * NU))
                        load_unit(it * 2 + h, u, h * NU + u)
            sp.wait_ge(s_out, 16 * NC)

        @block.gpsimd
        def _(pool):
            nc.gpsimd.memset(eps[:, :], EPS).then_inc(s_const, 1)
            nc.gpsimd.memset(zero[:, :], 0.0).then_inc(s_const, 1)
            nc.gpsimd.memset(ones[:, :], 1.0).then_inc(s_const, 1)
            nc.gpsimd.memset(ident[:, :], 0.0).then_inc(s_const, 1)
            pool.wait_ge(s_const, 4)
            nc.gpsimd.affine_select(out=ident[:, :], in_=ident[:, :], compare_op=ALU.not_equal, fill=1.0, base=0,
                                    pattern=[[-1, P]], channel_multiplier=1).then_inc(s_const, 1)

        @block.scalar
        def _(act):
            act.dma_start(w_ts[:, :], w_t).then_inc(s_w, 16)
            act.dma_start(w1s[:, :], w1).then_inc(s_w, 16)
            act.dma_start(bs[:, :], b).then_inc(s_w, 16)
            act.dma_start(w2s[:, :].rearrange("c (k f) -> c k f", f=F), w2.rearrange("k c f -> c k f")).then_inc(s_w, 16)
            act.wait_ge(s_const, 5)

            def sum_rows(k):
                n = N - k * P
                act.wait_ge(s_nat[k % 2], 16 * (k // 2 + 1))
                nc.scalar.activation(nat[k % 2][:, 0:n], nat[k % 2][:, 0:n], ACT.Copy,
                                     accum_out=natsum[:, k:k + 1]).then_inc(s_natsum, 1)

            act.wait_ge(s_var, 1)
            nc.scalar.activation(tmp[:, 0, :], tmp[:, 4, :], ACT.Sqrt, bias=zero[:, 0:1]).then_inc(s_std, 1)
            sum_rows(0)
            for k in range(T):
                act.wait_ge(s_rows, k + 1)
                nc.scalar.activation(root[:, k:k + 1], rows[:, k:k + 1], ACT.Sqrt,
                                     bias=zero[:, 0:1]).then_inc(s_root, 1)
                act.wait_ge(s_coef, k + 1)
                if k >= 2:
                    act.wait_ge(s_step, k - 1)
                nc.scalar.activation(feat[:, k % 2, :], tile(xs, k), ACT.Relu, scale=coef[:, k % 2, 0:1],
                                     bias=coef[:, k % 2, 1:2]).then_inc(s_feat, 1)
                if k + 1 < T:
                    sum_rows(k + 1)

            act.wait_ge(s_step, T)
            for c in range(0, NC - 1, 2):
                nc.scalar.activation(prop_t[:, c * CH:(c + 1) * CH], ps[c][:, :], ACT.Copy).then_inc(s_evac, 1)
            act.wait_ge(s_evac, 4)
            act.wait_ge(s_evacv, 3)
            act.wait_ge(s_tail_added, T)

            def pass_wait(semaphore, value):
                act.wait_ge(semaphore, value)
                act.sem_inc(s_passed, 1)

            def prep(g, par, first):
                if not first:
                    pass_wait(s_y, g)
                nc.scalar.activation(prop_g[:, :], at(prop_t, g * CH, CH), ACT.Copy).then_inc(s_pg, 1)
                act.wait_ge(s_var2, g + 1)
                nc.scalar.activation(tmp[:, 0, 0:G], tmp[:, 4, 0:G], ACT.Sqrt, bias=zero[:, 0:1]).then_inc(s_std2, 1)
                if not first:
                    act.wait_ge(s_tr, g)
                pass_wait(s_ln2, g + 1)
                for t in range(G):
                    nc.scalar.activation(tile(h2, t), at(xs, g * CH + t * P, P), ACT.Relu, scale=ln2[:, t, 0:1],
                                         bias=ln2[:, t, 1:2]).then_inc(s_h2, 1)
                act.wait_ge(s_tr, g + 1)
                if not first:
                    act.wait_ge(s_prod, (g - 1) * (Q * G))
                nc.scalar.activation(h2t[:, par, :], ps_t[:, :], ACT.Copy).then_inc(s_h2t, 1)
                pass_wait(s_nodeps, g + 1)
                nc.scalar.activation(node_t[:, bass.ds(g * CH, CH)], ps_node_t[0:K, :], ACT.Copy).then_inc(s_node_t, 1)

            prep(0, 0, True)
            prep(1, 1, False)
            with act.Fori(1, NC // 2) as it:
                prep(it * 2, 0, False)
                prep(it * 2 + 1, 1, False)

            def finish(c, h):
                act.wait_ge(s_um, c * NU + NU)
                nc.scalar.activation(act2[:, h, :], ps[h][:, :], ACT.Relu).then_inc(s_relu, 1)
                act.wait_ge(s_res, c + 1)
                act.dma_start(out.rearrange("(t p) f -> p t f", p=P)[:, bass.ds(c * G, G), :],
                              at(xs, c * CH, CH).rearrange("p (t f) -> p t f", f=F)).then_inc(s_out, 16)

            with act.Fori(0, NC // 2) as it:
                finish(it * 2, 0)
                finish(it * 2 + 1, 1)

        @block.vector
        def _(dve):
            v = Steps(s_v)

            def then(instruction, step):
                step.inc(instruction)
                step.wait(dve)

            def variance(st, n, step):
                total, gap, sq, var = tmp[:, 1, 0:n], tmp[:, 2, 0:n], tmp[:, 3, 0:n], tmp[:, 4, 0:n]
                step.inc(nc.vector.tensor_tensor(total, st[:, 0:n, 1], st[:, 0:n, 4], ALU.add))
                step.inc(nc.vector.tensor_tensor(gap, st[:, 0:n, 1], st[:, 0:n, 4], ALU.subtract))
                then(nc.vector.tensor_tensor(sq, st[:, 0:n, 2], st[:, 0:n, 5], ALU.add), step)
                then(nc.vector.tensor_scalar(sq, sq, 1.0 / F, EPS, ALU.mult, ALU.add), step)
                then(nc.vector.tensor_tensor(gap, gap, gap, ALU.mult), step)
                return nc.vector.scalar_tensor_tensor(out=var, in0=gap, scalar=0.25, in1=sq, op0=ALU.mult, op1=ALU.add)

            def inverse_root(square, rt, dst, s, step):
                then(nc.vector.reciprocal(dst, rt), step)
                then(nc.vector.tensor_tensor(s, dst, dst, ALU.mult), step)
                then(nc.vector.tensor_tensor(s, s, square, ALU.mult), step)
                then(nc.vector.tensor_scalar(s, s, -0.5, 1.5, ALU.mult, ALU.add), step)
                then(nc.vector.tensor_tensor(dst, dst, s, ALU.mult), step)

            def ln_scales(n, dst, step):
                rstd = tmp[:, 0, 0:n]
                inverse_root(tmp[:, 4, 0:n], tmp[:, 0, 0:n], tmp[:, 2, 0:n], tmp[:, 3, 0:n], step)
                rstd = tmp[:, 2, 0:n]
                step.inc(nc.vector.tensor_copy(dst[:, 0:n, 0], rstd))
                return nc.vector.scalar_tensor_tensor(out=dst[:, 0:n, 1], in0=tmp[:, 1, 0:n], scalar=-0.5, in1=rstd,
                                                      op0=ALU.mult, op1=ALU.mult)

            dve.wait_ge(s_x, 16)
            for t in range(T):
                v.inc(nc.vector.bn_stats(stats[:, t, :], tile(xs, t)))
            v.wait(dve)
            variance(stats, T, v).then_inc(s_var, 1)
            dve.wait_ge(s_std, 1)
            then(ln_scales(T, ln, v), v)

            def degree(k):
                dve.wait_ge(s_natsum, k + 1)
                if k == 0:
                    nc.vector.tensor_copy(rows[:, 0:1], natsum[:, 0:1]).then_inc(s_rows, 1)
                else:
                    dve.wait_ge(s_rowps, k)
                    nc.vector.tensor_tensor(rows[:, k:k + 1], psrow, natsum[:, k:k + 1], ALU.add).then_inc(s_rows, 1)
                dve.wait_ge(s_root, k + 1)
                inverse_root(rows[:, k:k + 1], root[:, k:k + 1], deg[:, k:k + 1], dnew[:, 0:1], v)
                if k >= 2:
                    dve.wait_ge(s_feat, k - 1)
                nc.vector.tensor_scalar(coef[:, k % 2, :], ln[:, k, :], deg[:, k:k + 1], None,
                                        ALU.mult).then_inc(s_coef, 1)

            degree(0)
            tail_sum = prop_t[:, N - CH:N]
            for k in range(T):
                strip = ring[k % R]
                dve.wait_ge(s_ring[k % R], 16 * (k // R + 1))
                if k + 1 < T:
                    if k == 0:
                        ins = nc.vector.tensor_copy(part_blk[:, 1, :], tile(strip, 1))
                    else:
                        v.wait(dve)
                        if k >= 2:
                            dve.wait_ge(s_rowps, k - 1)
                        ins = nc.vector.tensor_tensor(part_blk[:, (k + 1) % 2, :], tile(part, k + 1),
                                                      tile(strip, k + 1), ALU.add)
                    ins.then_inc(s_part, 1)
                if k + 2 < T:
                    rest = slice((k + 2) * P, N)
                    if k == 0:
                        v.inc(nc.vector.tensor_copy(part[:, rest], strip[:, rest]))
                    else:
                        v.inc(nc.vector.tensor_tensor(part[:, rest], part[:, rest], strip[:, rest], ALU.add))
                dve.wait_ge(s_tail, k + 1)
                if k == 0:
                    nc.vector.tensor_copy(tail_sum, tail[:, :]).then_inc(s_tail_added, 1)
                else:
                    dve.wait_ge(s_tail_added, k)
                    nc.vector.tensor_tensor(tail_sum, tail_sum, tail[:, :], ALU.add).then_inc(s_tail_added, 1)
                v.wait(dve)
                dve.wait_ge(s_part, min(k + 1, T - 1))
                dve.sem_inc(s_strip_read, 1)
                if k + 1 < T:
                    degree(k + 1)

            dve.wait_ge(s_step, T)
            for c in range(1, NC - 1, 2):
                nc.vector.tensor_copy(prop_t[:, c * CH:(c + 1) * CH], ps[c][:, :]).then_inc(s_evacv, 1)

            def prep_x1(g, step):
                dve.wait_ge(s_y, g + 1)
                for t in range(G):
                    xt = at(xs, g * CH + t * P, P)
                    step.inc(nc.vector.scalar_tensor_tensor(out=xt, in0=tile(ps_y, t), scalar=at(deg, g * G + t, 1),
                                                            in1=xt, op0=ALU.mult, op1=ALU.add))
                step.wait(dve)
                dve.sem_inc(s_x1, 1)
                for t in range(G):
                    step.inc(nc.vector.bn_stats(stats[:, t, :], at(xs, g * CH + t * P, P)))
                step.wait(dve)
                variance(stats, G, step).then_inc(s_var2, 1)
                dve.wait_ge(s_std2, g + 1)
                then(ln_scales(G, ln2, step), step)
                dve.sem_inc(s_ln2, 1)

            def prep_node(g, par):
                dve.wait_ge(s_nodeps, g + 1)
                nc.vector.tensor_copy(node[:, par, :], ps_node[:, 0:G * K]).then_inc(s_node, 1)

            def combine(g, par, t, step):
                for q in range(Q):
                    dve.wait_ge(s_prod, g * (Q * G) + (t * Q + q + 1))
                    if q == 0:
                        dve.wait_ge(s_node, g + 1)
                    for kk in range(KQ):
                        k = q * KQ + kk
                        src = ps[q][:, kk * F:(kk + 1) * F]
                        nd = node[:, par, t * K + k:t * K + k + 1]
                        o = mix[:, t % 2, :]
                        if k == 0:
                            then(nc.vector.tensor_scalar(o, src, nd, None, ALU.mult), step)
                            continue
                        dst = at(mixed, g * CH + t * P, P) if k == K - 1 else o
                        ins = nc.vector.scalar_tensor_tensor(out=dst, in0=src, scalar=nd, in1=o, op0=ALU.mult,
                                                             op1=ALU.add)
                        if kk < KQ - 1:
                            then(ins, step)
                        else:
                            ins.then_inc(s_prod_read, 1)
                            dve.wait_ge(s_prod_read, g * (Q * G) + (t * Q + q + 1))

            def group(g, par, step, last=False):
                combine(g, par, 0, step)
                if not last:
                    prep_x1(g + 1, step)
                combine(g, par, 1, step)
                combine(g, par, 2, step)
                if not last:
                    prep_node(g + 1, 1 - par)
                combine(g, par, 3, step)

            prep_x1(0, v)
            prep_node(0, 0)
            base = v.n
            with dve.Fori(0, NC // 2 - 1) as it:
                per = 2 * (G * (K - Q) + PREP)
                step = Steps(s_v, it * per + base)
                group(it * 2, 0, step)
                group(it * 2 + 1, 1, step)
                assert step.n == per, (step.n, per)
            step = Steps(s_v, base + per * (NC // 2 - 1))
            group(NC - 2, 0, step)
            group(NC - 1, 1, step, last=True)

            def add_back(c, h):
                dve.wait_ge(s_back, c + 1)
                nc.vector.tensor_tensor(at(xs, c * CH, CH), ps[2 + h][:, :], at(xs, c * CH, CH),
                                        ALU.add).then_inc(s_res, 1)

            with dve.Fori(0, NC // 2) as it:
                add_back(it * 2, 0)
                add_back(it * 2 + 1, 1)

        @block.tensor
        def _(pe):
            pe.wait_ge(s_const, 5)

            def step1(k, j, first=False, last=False):
                f = feat[:, j % 2, :]
                strip = ring[j]
                pe.wait_ge(s_feat, k + 1)
                nc.tensor.matmul(tail[:, :], f, strip[:, N - CH:N], start=True, stop=True).then_inc(s_tail, 1)
                for c in range(NC - 1):
                    if c == 3 and not last:
                        pe.wait_ge(s_part, k + 1)
                        pe.wait_ge(s_tail_added, k + 1)
                        nc.tensor.matmul(psrow, part_blk[:, (j + 1) % 2, :], ones[:, 0:1], start=True,
                                         stop=True).then_inc(s_rowps, 1)
                    ins = nc.tensor.matmul(ps[c][:, :], f, strip[:, c * CH:(c + 1) * CH], start=first, stop=last)
                ins.then_inc(s_step, 1)

            for k in range(R):
                pe.wait_ge(s_ring[k], 16)
                step1(k, k, first=(k == 0))
            with pe.Fori(1, T // R - 1) as it:
                for j in range(R):
                    pe.wait_ge(s_ring[j], it * 16 + 16)
                    step1(it * R + j, j)
            for j in range(R):
                pe.wait_ge(s_ring[j], 16 * (T // R))
                step1(T - R + j, j, last=(j == R - 1))

            pe.wait_ge(s_w, 64)

            def y_product(g, first=False):
                if not first:
                    pe.wait_ge(s_x1, g)
                pe.wait_ge(s_pg, g + 1)
                for t in range(G):
                    ins = nc.tensor.matmul(tile(ps_y, t), tile(prop_g, t), w_ts[:, :], start=True, stop=True)
                ins.then_inc(s_y, 1)

            def transposes(g):
                pe.wait_ge(s_h2, (g + 1) * G)
                for t in range(G):
                    ins = nc.tensor.transpose(tile(ps_t, t), tile(h2, t), ident[:, :])
                ins.then_inc(s_tr, 1)

            def nodes(g, par, first=False):
                if not first:
                    pe.wait_ge(s_node_t, g)
                pe.wait_ge(s_h2t, g + 1)
                for t in range(G):
                    nc.tensor.matmul(ps_node[:, t * K:(t + 1) * K], tile(h2t[:, par, :], t), w1s[:, :],
                                     start=True, stop=True)
                nc.tensor.matmul(ps_node_t[0:K, :], w1s[:, :], h2t[:, par, :], start=True, stop=True)\
                    .then_inc(s_nodeps, 1)

            def mix_products(g, par, t, first=False):
                for q in range(Q):
                    if not (first and t == 0):
                        pe.wait_ge(s_prod_read, g * (Q * G) + ((t - 1) * Q + q + 1))
                    nc.tensor.matmul(ps[q][:, :], tile(h2t[:, par, :], t), w2s[:, q * CH:(q + 1) * CH],
                                     start=True, stop=True).then_inc(s_prod, 1)

            def group(g, par, first=False, last=False):
                if not last:
                    y_product(g + 1)
                mix_products(g, par, 0, first)
                mix_products(g, par, 1)
                if not last:
                    transposes(g + 1)
                mix_products(g, par, 2)
                if not last:
                    nodes(g + 1, 1 - par)
                mix_products(g, par, 3)

            y_product(0, first=True)
            transposes(0)
            nodes(0, 0, first=True)
            group(0, 0, first=True)
            group(1, 1)
            with pe.Fori(1, NC // 2 - 1) as it:
                group(it * 2, 0)
                group(it * 2 + 1, 1)
            group(NC - 2, 0)
            group(NC - 1, 1, last=True)

            pe.wait_ge(s_prod_read, T * Q)
            pe.wait_ge(s_node_t, NC)

            def back(c, h, bank_used=True):
                if bank_used:
                    pe.wait_ge(s_res, c - 1)
                pe.wait_ge(s_relu, c + 1)
                for t in range(G):
                    ins = nc.tensor.transpose(tile(ps[2 + h], t), tile(act2[:, h, :], t), ident[:, :])
                ins.then_inc(s_back, 1)

            def chunk(c, h, uses, first=False, bank_used=True):
                nc.tensor.matmul(ps[h][:, :], bs[:, :], node_t[:, bass.ds(c * CH, CH)], start=True, stop=False)
                for u in range(NU):
                    pe.wait_ge(s_unit[h * NU + u], uses)
                    for j in range(UJ):
                        ins = nc.tensor.matmul(ps[h][:, :], tile(mixed, u * UJ + j), unit[h * NU + u][:, j, :],
                                               start=False, stop=(u == NU - 1 and j == UJ - 1))
                    ins.then_inc(s_um, 1)
                    if u == 1 and not first:
                        back(c - 1, 1 - h, bank_used)

            chunk(0, 0, 16, first=True)
            chunk(1, 1, 16, bank_used=False)
            chunk(2, 0, 32, bank_used=False)
            chunk(3, 1, 32)
            with pe.Fori(2, NC // 2) as it:
                chunk(it * 2, 0, it * 16 + 16)
                chunk(it * 2 + 1, 1, it * 16 + 16)
            back(NC - 1, 1)


PREP = 4 + 4 + 5 + 5 + 2


def kernel(x, adj, L0_gnn_W, L1_gnn_W1, L1_gnn_W2, L1_gnn_b):
    import numpy as np
    import concourse.bacc as bacc
    from concourse.bass_utils import run_bass_kernel_spmd

    adj = np.asarray(adj)
    arrays = {
        "x": np.ascontiguousarray(x),
        "adj": np.ascontiguousarray(adj),
        "adj_t": np.ascontiguousarray(adj.T),
        "w_t": np.ascontiguousarray(np.asarray(L0_gnn_W).T),
        "w1": np.ascontiguousarray(L1_gnn_W1),
        "w2": np.ascontiguousarray(L1_gnn_W2),
        "b": np.ascontiguousarray(L1_gnn_b),
    }
    nc = bacc.Bacc("TRN2", target_bir_lowering=False, num_devices=1)
    args = [nc.dram_tensor(n, a.shape, mybir.dt.from_np(a.dtype), kind="ExternalInput").ap() for n, a in arrays.items()]
    out = nc.dram_tensor("out", arrays["x"].shape, F32, kind="ExternalOutput").ap()
    two_graph_layers(nc, *args, out)
    result = run_bass_kernel_spmd(nc, [arrays], core_ids=[0])
    return result.results[0]["out"]
```

```python
from contextlib import ExitStack

import concourse.bass as bass
from concourse import mybir

P = 128
ALU = mybir.AluOpType
ACT = mybir.ActivationFunctionType
F32 = mybir.dt.float32
F32R = mybir.dt.float32r


class Steps:

    def __init__(self, sem, base=0):
        self.sem, self.base, self.n = sem, base, 0

    def inc(self, instruction):
        instruction.then_inc(self.sem, 1)
        self.n += 1

    def wait(self, eng):
        eng.wait_ge(self.sem, self.base + self.n)


def two_graph_layers(nc, x_in, adj, adj_t, w_t, w1, w2, b, out):
    N, F = x_in.shape
    K = w1.shape[1]
    T = N // P
    CH = 512
    NC = N // CH
    G = CH // P
    R = 4
    KQ = CH // F
    Q = K // KQ
    UJ = 4
    NU = T // UJ
    EPS = 1e-5
    assert F == P and NC == 8 and NU == 8 and T % R == 0

    with ExitStack() as ctx:
        def sb(name, shape, dtype=F32):
            return ctx.enter_context(nc.sbuf_tensor(name, shape, dtype))

        def sem(name):
            return ctx.enter_context(nc.semaphore(name))

        def alloc(stack, name, shape, dtype=F32):
            return stack.enter_context(nc.sbuf_tensor(name, shape, dtype))

        xs = sb("xs", [P, N])
        prop_t = sb("prop_t", [P, N])
        node_t = prop_t[0:K, :]
        w2_raw = prop_t[:, 0:K * F]
        part_blk = sb("part_blk", [P, 2, P])
        feat = sb("feat", [P, 2, F])
        w_ts = sb("w_ts", [P, F])
        w1_raw = sb("w1_raw", [P, K])
        bs = sb("bs", [K, F])
        ident = sb("ident", [P, P])
        ones = sb("ones", [P, 2])
        eps = sb("eps", [P, 1])
        zero = sb("zero", [P, 1])
        stats = sb("stats", [P, T, 6])
        tmp = sb("tmp", [P, 5, T])
        ln = sb("ln", [P, T, 2])
        natsum = sb("natsum", [P, T])
        rows = sb("rows", [P, T])
        root = sb("root", [P, T])
        dnew = sb("dnew", [P, 2])
        deg = sb("deg", [P, T])
        coef = sb("coef", [P, 2, 2])
        ln2 = sb("ln2", [P, G, 2])
        node = sb("node", [P, 2, G * K])
        act2 = sb("act2", [P, 2, CH])
        with ExitStack() as early:
            w2_hi = alloc(early, "w2_hi", [P, K * F], F32R)
            w2_lo = alloc(early, "w2_lo", [P, K * F], F32R)
            w1_hi = alloc(early, "w1_hi", [P, P], F32R)
            w1_lo = alloc(early, "w1_lo", [P, P], F32R)
            prop_g = alloc(early, "prop_g", [P, CH])
            h2 = alloc(early, "h2", [P, CH])
            h2_hi = alloc(early, "h2_hi", [P, 2, CH], F32R)
            h2_lo = alloc(early, "h2_lo", [P, 2, CH], F32R)
            prods = alloc(early, "prods", [P, G, 2 * KQ * F])
        adj_hi = sb("adj_hi", [P, 2, UJ * CH], F32R)
        adj_lo = sb("adj_lo", [P, 2, UJ * CH], F32R)
        stage_2 = 2 * K * F + 2 * P + 6 * CH + 2 * G * KQ * F
        sb("rest_of_stage_2_buffers", [P, stage_2 - 4 * UJ * CH])
        with ExitStack() as early:
            pieces = alloc(early, "pieces", [P, (R + 2) * N])
            part = alloc(early, "part", [P, N])
        ring = [pieces[:, s * N:(s + 1) * N] for s in range(R)]
        nat = [pieces[:, (R + s) * N:(R + s + 1) * N] for s in range(2)]
        units = sb("units", [P, NU * UJ * CH])
        unit = [units[:, s * UJ * CH:(s + 1) * UJ * CH] for s in range(NU)]
        accs = sb("accs", [P, G, KQ * F])
        mixed_hi = sb("mixed_hi", [P, N], F32R)
        mixed_lo = sb("mixed_lo", [P, N], F32R)
        ps = [ctx.enter_context(nc.psum_tensor(f"ps{i}", [P, CH], F32)) for i in range(8)]
        tail, psrow = ps[7], ps[7][:, 0:1]
        ps_y, ps_node = ps[6], ps[6]
        ps_t, ps_node_t = ps[7], ps[7]

        def mix_bank(q, t):
            return ps[q + 2 * (t % 2)] if q >= 2 else ps[q]

        def scalar_banks(t):
            return [0] if t == 0 else [0, 1]

        s_x = sem("x_landed")
        s_w = sem("weights_landed")
        s_nat = [sem(f"nat_landed{i}") for i in range(2)]
        s_ring = [sem(f"strip_landed{i}") for i in range(R)]
        s_unit = [sem(f"unit_landed{i}") for i in range(NU)]
        s_const = sem("constants_set")
        s_natsum = sem("natural_part_summed")
        s_part = sem("part_block_ready")
        s_strip_read = sem("strip_read_by_vector")
        s_tail = sem("tail_product_ready")
        s_tail_added = sem("tail_added")
        s_rowps = sem("rowsum_in_psum")
        s_rows = sem("rowsum_ready")
        s_root = sem("root_ready")
        s_coef = sem("coefficients_ready")
        s_feat = sem("features_ready")
        s_step = sem("step_multiplied")
        s_v = sem("vector_steps")
        s_var = sem("variance_ready")
        s_std = sem("std_ready")
        s_evac = sem("propagated_out_of_psum_by_scalar")
        s_evacv = sem("propagated_out_of_psum_by_vector")
        s_pg = sem("propagated_group_copied")
        s_y = sem("y_ready")
        s_x1 = sem("x1_ready")
        s_passed = sem("scalar_wait_passed")
        s_var2 = sem("variance2_ready")
        s_std2 = sem("std2_ready")
        s_ln2 = sem("ln2_ready")
        s_h2 = sem("h2_ready")
        s_tr = sem("h2_transposed")
        s_h2t = sem("h2t_copied")
        s_nodeps = sem("node_in_psum")
        s_node = sem("node_copied")
        s_node_t = sem("node_t_copied")
        s_prod = sem("mix_products_ready")
        s_bank = [sem(f"mix_bank_read{q}") for q in range(Q)]
        s_pool = sem("pool_steps")
        s_sum = sem("tile_sums_read")
        s_mixed = sem("mixed_ready")
        s_w_split = sem("weights_hi_ready")
        s_w_lo = sem("weights_lo_ready")
        s_h2t_lo = sem("h2t_lo_ready")
        s_hi = sem("unit_hi_ready")
        s_lo = sem("unit_lo_ready")
        s_pass = sem("pool_wait_passed")
        s_um = sem("unit_multiplied")
        s_relu = sem("chunk_activated")
        s_back = sem("chunk_transposed_back")
        s_res = sem("chunk_result_ready")
        s_out = sem("result_stored")

        block = ctx.enter_context(nc.Block())
        adj_u = adj_t.rearrange("(u j p) i -> u p j i", j=UJ, p=P)

        def tile(buf, t):
            return buf[:, t * P:(t + 1) * P]

        def at(buf, start, size):
            return buf[:, bass.ds(start, size)]

        @block.sync
        def _(sp):
            def load_rows(k):
                if k >= 2:
                    sp.wait_ge(s_natsum, k - 1)
                sp.dma_start(nat[k % 2][:, 0:N - k * P], adj[k * P:(k + 1) * P, k * P:N]).then_inc(s_nat[k % 2], 16)

            load_rows(0)
            sp.dma_start(xs[:, :].rearrange("p (t f) -> p t f", f=F),
                         x_in.rearrange("(t p) f -> p t f", p=P)).then_inc(s_x, 16)
            for k in range(T):
                if k >= R:
                    sp.wait_ge(s_step, k - R + 1)
                    sp.wait_ge(s_strip_read, k - R + 1)
                sp.dma_start(ring[k % R], adj_t[k * P:(k + 1) * P, :]).then_inc(s_ring[k % R], 16)
                if k + 1 < T:
                    load_rows(k + 1)

            def load_unit(c, u):
                sp.dma_start(unit[u].rearrange("p (j i) -> p j i", j=UJ),
                             adj_u[u][:, :, bass.ds(c * CH, CH)]).then_inc(s_unit[u], 16)

            sp.wait_ge(s_step, T)
            sp.wait_ge(s_strip_read, T)
            for u in range(NU):
                load_unit(0, u)
            with sp.Fori(1, NC) as c:
                for u in range(NU):
                    sp.wait_ge(s_lo, c * NU + (u + 1 - NU))
                    load_unit(c, u)
            sp.wait_ge(s_out, 16 * NC)

        @block.gpsimd
        def _(pool):
            nc.gpsimd.memset(eps[:, :], EPS).then_inc(s_const, 1)
            nc.gpsimd.memset(zero[:, :], 0.0).then_inc(s_const, 1)
            nc.gpsimd.memset(w1_hi[:, K:P].bitcast(F32), 0.0).then_inc(s_const, 1)
            nc.gpsimd.memset(w1_lo[:, K:P].bitcast(F32), 0.0).then_inc(s_const, 1)
            nc.gpsimd.memset(ones[:, :], 1.0).then_inc(s_const, 1)
            nc.gpsimd.memset(ident[:, :], 0.0).then_inc(s_const, 1)
            pool.wait_ge(s_const, 6)
            nc.gpsimd.affine_select(out=ident[:, :], in_=ident[:, :], compare_op=ALU.not_equal, fill=1.0, base=0,
                                    pattern=[[-1, P]], channel_multiplier=1).then_inc(s_const, 1)

            def merge(g, t, step):
                idx = g * G + t
                p, a = prods[:, t, :], accs[:, t, :]
                pool.wait_ge(s_bank[Q - 1], idx + 1)
                if len(scalar_banks(t)) > 1:
                    pool.wait_ge(s_bank[1], idx + 1)
                    step.inc(nc.gpsimd.tensor_tensor(a, a, p[:, CH:2 * CH], ALU.add))
                    step.wait(pool)
                step.inc(nc.gpsimd.tensor_tensor(a[:, 0:2 * F], a[:, 0:2 * F], a[:, 2 * F:4 * F], ALU.add))
                step.wait(pool)
                step.inc(nc.gpsimd.tensor_tensor(a[:, 0:F], a[:, 0:F], a[:, F:2 * F], ALU.add))
                pool.wait_ge(step.sem, step.base + step.n)
                pool.sem_inc(s_pass, 1)
                dst = bass.ds(g * CH + t * P, P)
                step.inc(nc.gpsimd.tensor_copy(mixed_hi[:, dst], a[:, 0:F]))
                pool.wait_ge(step.sem, step.base + step.n)
                pool.sem_inc(s_pass, 1)
                nc.gpsimd.tensor_tensor(mixed_lo[:, dst], a[:, 0:F], mixed_hi[:, dst].bitcast(F32),
                                        ALU.subtract).then_inc(s_mixed, 1)

            with pool.Fori(0, NC) as g:
                per = sum(2 + len(scalar_banks(t)) for t in range(G))
                step = Steps(s_pool, g * per)
                for t in range(G):
                    merge(g, t, step)
                assert step.n == per
        @block.scalar
        def _(act):
            act.dma_start(w_ts[:, :], w_t).then_inc(s_w, 16)
            act.dma_start(w1_raw[:, :], w1).then_inc(s_w, 16)
            act.dma_start(bs[:, :], b).then_inc(s_w, 16)
            act.dma_start(w2_raw.rearrange("c (k f) -> c k f", f=F), w2.rearrange("k c f -> c k f")).then_inc(s_w, 16)
            act.wait_ge(s_const, 7)

            def sum_rows(k):
                n = N - k * P
                act.wait_ge(s_nat[k % 2], 16 * (k // 2 + 1))
                nc.scalar.activation(nat[k % 2][:, 0:n], nat[k % 2][:, 0:n], ACT.Copy,
                                     accum_out=natsum[:, k:k + 1]).then_inc(s_natsum, 1)

            act.wait_ge(s_var, 1)
            nc.scalar.activation(tmp[:, 0, :], tmp[:, 4, :], ACT.Sqrt, bias=zero[:, 0:1]).then_inc(s_std, 1)
            sum_rows(0)
            for k in range(T):
                act.wait_ge(s_rows, k + 1)
                nc.scalar.activation(root[:, k:k + 1], rows[:, k:k + 1], ACT.Sqrt,
                                     bias=zero[:, 0:1]).then_inc(s_root, 1)
                act.wait_ge(s_coef, k + 1)
                if k >= 2:
                    act.wait_ge(s_step, k - 1)
                nc.scalar.activation(feat[:, k % 2, :], tile(xs, k), ACT.Relu, scale=coef[:, k % 2, 0:1],
                                     bias=coef[:, k % 2, 1:2]).then_inc(s_feat, 1)
                if k + 1 < T:
                    sum_rows(k + 1)
                if k == T // 2:
                    act.wait_ge(s_w, 64)
                    nc.scalar.activation(w2_hi[:, :], w2_raw, ACT.Copy).then_inc(s_w_split, 1)
                    nc.scalar.activation(w1_hi[:, 0:K], w1_raw[:, :], ACT.Copy).then_inc(s_w_split, 1)

            act.wait_ge(s_w_lo, 2)
            act.wait_ge(s_step, T)
            for c in range(0, NC - 1, 2):
                nc.scalar.activation(prop_t[:, c * CH:(c + 1) * CH], ps[c][:, :], ACT.Copy).then_inc(s_evac, 1)
            act.wait_ge(s_evac, 4)
            act.wait_ge(s_evacv, 3)
            act.wait_ge(s_tail_added, T)

            def pass_wait(semaphore, value):
                act.wait_ge(semaphore, value)
                act.sem_inc(s_passed, 1)

            def copy_group(g, first=False):
                if not first:
                    pass_wait(s_y, g)
                nc.scalar.activation(prop_g[:, :], at(prop_t, g * CH, CH), ACT.Copy).then_inc(s_pg, 1)

            def std(g):
                act.wait_ge(s_var2, g + 1)
                nc.scalar.activation(tmp[:, 0, 0:G], tmp[:, 4, 0:G], ACT.Sqrt, bias=zero[:, 0:1]).then_inc(s_std2, 1)

            def normed(g, first=False):
                if not first:
                    act.wait_ge(s_tr, g)
                pass_wait(s_ln2, g + 1)
                for t in range(G):
                    nc.scalar.activation(tile(h2, t), at(xs, g * CH + t * P, P), ACT.Relu, scale=ln2[:, t, 0:1],
                                         bias=ln2[:, t, 1:2]).then_inc(s_h2, 1)

            def high_part(g, par, slot_used=True):
                act.wait_ge(s_tr, g + 1)
                if slot_used:
                    act.wait_ge(s_prod, (g - 1) * (Q * G))
                nc.scalar.activation(h2_hi[:, par, :], ps_t[:, :], ACT.Copy).then_inc(s_h2t, 1)

            def copy_node_t(g):
                pass_wait(s_nodeps, g + 1)
                nc.scalar.activation(node_t[:, bass.ds(g * CH, CH)], ps_node_t[0:K, :], ACT.Copy).then_inc(s_node_t, 1)

            def products(g, par, t, first=False):
                idx = g * G + t
                if not first:
                    act.wait_ge(s_mixed, idx - G + 1)
                act.wait_ge(s_node, g + 1)
                for q in scalar_banks(t):
                    act.wait_ge(s_prod, g * (Q * G) + (t * Q + q + 1))
                    for kk in range(KQ):
                        k = q * KQ + kk
                        ins = nc.scalar.activation(prods[:, t, k * F:(k + 1) * F], mix_bank(q, t)[:, kk * F:(kk + 1) * F],
                                                   ACT.Copy, scale=node[:, par, t * K + k:t * K + k + 1])
                    ins.then_inc(s_bank[q], 1)

            def group(g, par, first=False, more=2, slot_used=True):
                if more > 1:
                    copy_group(g + 2)
                products(g, par, 0, first)
                if more > 0:
                    normed(g + 1)
                products(g, par, 1, first)
                if more > 0:
                    high_part(g + 1, 1 - par, slot_used)
                products(g, par, 2, first)
                if more > 1:
                    std(g + 2)
                products(g, par, 3, first)
                if more > 0:
                    copy_node_t(g + 1)

            copy_group(0, first=True)
            std(0)
            normed(0, first=True)
            copy_group(1)
            high_part(0, 0, slot_used=False)
            std(1)
            copy_node_t(0)
            group(0, 0, first=True, slot_used=False)
            group(1, 1)
            with act.Fori(1, NC // 2 - 1) as it:
                group(it * 2, 0)
                group(it * 2 + 1, 1)
            group(NC - 2, 0, more=1)
            group(NC - 1, 1, more=0)

            act.wait_ge(s_prod, Q * T)

            def activate(c, h):
                act.wait_ge(s_um, c * NU + NU)
                nc.scalar.activation(act2[:, h, :], ps[h][:, :], ACT.Relu).then_inc(s_relu, 1)

            def store(c):
                act.wait_ge(s_res, c + 1)
                act.dma_start(out.rearrange("(t p) f -> p t f", p=P)[:, bass.ds(c * G, G), :],
                              at(xs, c * CH, CH).rearrange("p (t f) -> p t f", f=F)).then_inc(s_out, 16)

            def chunk(c, h, first=False):
                for u in range(NU):
                    if not (first and u < 2):
                        act.wait_ge(s_um, c * NU + (u - 1))
                    act.wait_ge(s_unit[u], c * 16 + 16)
                    nc.scalar.activation(adj_hi[:, u % 2, :], unit[u], ACT.Copy).then_inc(s_hi, 1)
                    if u == 1 and not first:
                        activate(c - 1, 1 - h)
                    if u == 5 and not first:
                        store(c - 1)

            chunk(0, 0, first=True)
            chunk(1, 1)
            with act.Fori(1, NC // 2) as it:
                chunk(it * 2, 0)
                chunk(it * 2 + 1, 1)
            activate(NC - 1, 1)
            store(NC - 1)

        @block.vector
        def _(dve):
            v = Steps(s_v)

            def then(instruction, step):
                step.inc(instruction)
                step.wait(dve)

            def variance(st, n, step):
                total, gap, sq, var = tmp[:, 1, 0:n], tmp[:, 2, 0:n], tmp[:, 3, 0:n], tmp[:, 4, 0:n]
                step.inc(nc.vector.tensor_tensor(total, st[:, 0:n, 1], st[:, 0:n, 4], ALU.add))
                step.inc(nc.vector.tensor_tensor(gap, st[:, 0:n, 1], st[:, 0:n, 4], ALU.subtract))
                then(nc.vector.tensor_tensor(sq, st[:, 0:n, 2], st[:, 0:n, 5], ALU.add), step)
                then(nc.vector.tensor_scalar(sq, sq, 1.0 / F, EPS, ALU.mult, ALU.add), step)
                then(nc.vector.tensor_tensor(gap, gap, gap, ALU.mult), step)
                return nc.vector.scalar_tensor_tensor(out=var, in0=gap, scalar=0.25, in1=sq, op0=ALU.mult, op1=ALU.add)

            def inverse_root(square, rt, dst, s, step):
                then(nc.vector.reciprocal(dst, rt), step)
                then(nc.vector.tensor_tensor(s, dst, dst, ALU.mult), step)
                then(nc.vector.tensor_tensor(s, s, square, ALU.mult), step)
                then(nc.vector.tensor_scalar(s, s, -0.5, 1.5, ALU.mult, ALU.add), step)
                then(nc.vector.tensor_tensor(dst, dst, s, ALU.mult), step)

            def ln_scales(n, dst, step):
                rstd = tmp[:, 0, 0:n]
                inverse_root(tmp[:, 4, 0:n], tmp[:, 0, 0:n], tmp[:, 2, 0:n], tmp[:, 3, 0:n], step)
                rstd = tmp[:, 2, 0:n]
                step.inc(nc.vector.tensor_copy(dst[:, 0:n, 0], rstd))
                return nc.vector.scalar_tensor_tensor(out=dst[:, 0:n, 1], in0=tmp[:, 1, 0:n], scalar=-0.5, in1=rstd,
                                                      op0=ALU.mult, op1=ALU.mult)

            dve.wait_ge(s_x, 16)
            for t in range(T):
                v.inc(nc.vector.bn_stats(stats[:, t, :], tile(xs, t)))
            v.wait(dve)
            variance(stats, T, v).then_inc(s_var, 1)
            dve.wait_ge(s_std, 1)
            then(ln_scales(T, ln, v), v)

            def degree(k):
                dve.wait_ge(s_natsum, k + 1)
                if k == 0:
                    nc.vector.tensor_copy(rows[:, 0:1], natsum[:, 0:1]).then_inc(s_rows, 1)
                else:
                    dve.wait_ge(s_rowps, k)
                    nc.vector.tensor_tensor(rows[:, k:k + 1], psrow, natsum[:, k:k + 1], ALU.add).then_inc(s_rows, 1)
                dve.wait_ge(s_root, k + 1)
                inverse_root(rows[:, k:k + 1], root[:, k:k + 1], deg[:, k:k + 1], dnew[:, 0:1], v)
                if k >= 2:
                    dve.wait_ge(s_feat, k - 1)
                nc.vector.tensor_scalar(coef[:, k % 2, :], ln[:, k, :], deg[:, k:k + 1], None,
                                        ALU.mult).then_inc(s_coef, 1)

            degree(0)
            tail_sum = prop_t[:, N - CH:N]
            for k in range(T):
                strip = ring[k % R]
                dve.wait_ge(s_ring[k % R], 16 * (k // R + 1))
                if k + 1 < T:
                    if k == 0:
                        ins = nc.vector.tensor_copy(part_blk[:, 1, :], tile(strip, 1))
                    else:
                        v.wait(dve)
                        if k >= 2:
                            dve.wait_ge(s_rowps, k - 1)
                        ins = nc.vector.tensor_tensor(part_blk[:, (k + 1) % 2, :], tile(part, k + 1),
                                                      tile(strip, k + 1), ALU.add)
                    ins.then_inc(s_part, 1)
                if k + 2 < T:
                    rest = slice((k + 2) * P, N)
                    if k == 0:
                        v.inc(nc.vector.tensor_copy(part[:, rest], strip[:, rest]))
                    else:
                        v.inc(nc.vector.tensor_tensor(part[:, rest], part[:, rest], strip[:, rest], ALU.add))
                dve.wait_ge(s_tail, k + 1)
                if k == 0:
                    nc.vector.tensor_copy(tail_sum, tail[:, :]).then_inc(s_tail_added, 1)
                else:
                    dve.wait_ge(s_tail_added, k)
                    nc.vector.tensor_tensor(tail_sum, tail_sum, tail[:, :], ALU.add).then_inc(s_tail_added, 1)
                v.wait(dve)
                dve.wait_ge(s_part, min(k + 1, T - 1))
                dve.sem_inc(s_strip_read, 1)
                if k + 1 < T:
                    degree(k + 1)
                if k == T // 2 + 1:
                    dve.wait_ge(s_w_split, 2)
                    nc.vector.tensor_tensor(w2_lo[:, :], w2_raw, w2_hi[:, :].bitcast(F32),
                                            ALU.subtract).then_inc(s_w_lo, 1)
                    nc.vector.tensor_tensor(w1_lo[:, 0:K], w1_raw[:, :], w1_hi[:, 0:K].bitcast(F32),
                                            ALU.subtract).then_inc(s_w_lo, 1)

            dve.wait_ge(s_step, T)
            for c in range(1, NC - 1, 2):
                nc.vector.tensor_copy(prop_t[:, c * CH:(c + 1) * CH], ps[c][:, :]).then_inc(s_evacv, 1)

            def prep_x1(g, step):
                dve.wait_ge(s_y, g + 1)
                for t in range(G):
                    xt = at(xs, g * CH + t * P, P)
                    step.inc(nc.vector.scalar_tensor_tensor(out=xt, in0=tile(ps_y, t), scalar=at(deg, g * G + t, 1),
                                                            in1=xt, op0=ALU.mult, op1=ALU.add))
                step.wait(dve)
                dve.sem_inc(s_x1, 1)

            def prep_var(g, step):
                for t in range(G):
                    step.inc(nc.vector.bn_stats(stats[:, t, :], at(xs, g * CH + t * P, P)))
                step.wait(dve)
                variance(stats, G, step).then_inc(s_var2, 1)

            def prep_ln(g, step):
                dve.wait_ge(s_std2, g + 1)
                then(ln_scales(G, ln2, step), step)
                dve.sem_inc(s_ln2, 1)

            def prep_lo(g, par):
                dve.wait_ge(s_h2t, g + 1)
                nc.vector.tensor_tensor(h2_lo[:, par, :], ps_t[:, :], h2_hi[:, par, :].bitcast(F32),
                                        ALU.subtract).then_inc(s_h2t_lo, 1)

            def copy_node(g, par):
                dve.wait_ge(s_nodeps, g + 1)
                nc.vector.tensor_copy(node[:, par, :], ps_node[:, 0:G * K]).then_inc(s_node, 1)

            def combine(g, par, t, step, first=False):
                idx = g * G + t
                if not first:
                    dve.wait_ge(s_mixed, idx - G + 1)
                dve.wait_ge(s_node, g + 1)
                dve.wait_ge(s_bank[0], idx + 1)
                mine = [q for q in range(Q) if q not in scalar_banks(t)]
                for q in mine:
                    dve.wait_ge(s_prod, g * (Q * G) + (t * Q + q + 1))
                    for kk in range(KQ):
                        k = q * KQ + kk
                        acc = accs[:, t, kk * F:(kk + 1) * F]
                        before = acc
                        if q == mine[0]:
                            before = prods[:, t, kk * F:(kk + 1) * F]
                        elif kk < KQ - 1:
                            dve.wait_ge(step.sem, step.base + (step.n - KQ + 2))
                        else:
                            dve.wait_ge(s_bank[q - 1], idx + 1)
                        ins = nc.vector.scalar_tensor_tensor(out=acc, in0=mix_bank(q, t)[:, kk * F:(kk + 1) * F],
                                                             scalar=node[:, par, t * K + k:t * K + k + 1],
                                                             in1=before, op0=ALU.mult, op1=ALU.add)
                        if kk < KQ - 1:
                            step.inc(ins)
                        else:
                            ins.then_inc(s_bank[q], 1)

            def group(g, par, step, first=False, more=2):
                combine(g, par, 0, step, first)
                combine(g, par, 1, step, first)
                if more > 1:
                    prep_x1(g + 2, step)
                if more > 0:
                    prep_lo(g + 1, 1 - par)
                if more > 1:
                    prep_var(g + 2, step)
                combine(g, par, 2, step, first)
                if more > 0:
                    copy_node(g + 1, 1 - par)
                if more > 1:
                    prep_ln(g + 2, step)
                combine(g, par, 3, step, first)

            prep_x1(0, v)
            prep_var(0, v)
            prep_ln(0, v)
            prep_x1(1, v)
            prep_var(1, v)
            prep_lo(0, 0)
            prep_ln(1, v)
            copy_node(0, 0)
            group(0, 0, v, first=True)
            per = 2 * ((KQ - 1) * sum(Q - len(scalar_banks(t)) for t in range(G)) + PREP)
            group(1, 1, v)
            base = v.n - per
            with dve.Fori(1, NC // 2 - 1) as it:
                step = Steps(s_v, it * per + base)
                group(it * 2, 0, step)
                group(it * 2 + 1, 1, step)
                assert step.n == per, (step.n, per)
            step = Steps(s_v, base + per * (NC // 2 - 1))
            group(NC - 2, 0, step, more=1)
            group(NC - 1, 1, step, more=0)

            dve.wait_ge(s_mixed, T)
            dve.wait_ge(s_prod, Q * T)
            def add_back(c, h):
                dve.wait_ge(s_back, c + 1)
                nc.vector.tensor_tensor(at(xs, c * CH, CH), ps[2 + h][:, :], at(xs, c * CH, CH),
                                        ALU.add).then_inc(s_res, 1)

            def chunk(c, h, first=False):
                for u in range(NU):
                    dve.wait_ge(s_hi, c * NU + (u + 1))
                    nc.vector.tensor_tensor(adj_lo[:, u % 2, :], unit[u], adj_hi[:, u % 2, :].bitcast(F32),
                                            ALU.subtract).then_inc(s_lo, 1)
                    if u == 3 and not first:
                        add_back(c - 1, 1 - h)

            chunk(0, 0, first=True)
            chunk(1, 1)
            with dve.Fori(1, NC // 2) as it:
                chunk(it * 2, 0)
                chunk(it * 2 + 1, 1)
            add_back(NC - 1, 1)

        @block.tensor
        def _(pe):
            pe.wait_ge(s_const, 7)

            def step1(k, j, first=False, last=False):
                f = feat[:, j % 2, :]
                strip = ring[j]
                pe.wait_ge(s_feat, k + 1)
                nc.tensor.matmul(tail[:, :], f, strip[:, N - CH:N], start=True, stop=True).then_inc(s_tail, 1)
                for c in range(NC - 1):
                    if c == 3 and not last:
                        pe.wait_ge(s_part, k + 1)
                        pe.wait_ge(s_tail_added, k + 1)
                        nc.tensor.matmul(psrow, part_blk[:, (j + 1) % 2, :], ones[:, 0:1], start=True,
                                         stop=True).then_inc(s_rowps, 1)
                    ins = nc.tensor.matmul(ps[c][:, :], f, strip[:, c * CH:(c + 1) * CH], start=first, stop=last)
                ins.then_inc(s_step, 1)

            for k in range(R):
                pe.wait_ge(s_ring[k], 16)
                step1(k, k, first=(k == 0))
            with pe.Fori(1, T // R - 1) as it:
                for j in range(R):
                    pe.wait_ge(s_ring[j], it * 16 + 16)
                    step1(it * R + j, j)
            for j in range(R):
                pe.wait_ge(s_ring[j], 16 * (T // R))
                step1(T - R + j, j, last=(j == R - 1))

            pe.wait_ge(s_w, 64)

            def y_product(g, first=False, node_used=True):
                if not first:
                    pe.wait_ge(s_x1, g)
                    if node_used:
                        pe.wait_ge(s_node, g - 1)
                pe.wait_ge(s_pg, g + 1)
                for t in range(G):
                    ins = nc.tensor.matmul(tile(ps_y, t), tile(prop_g, t), w_ts[:, :], start=True, stop=True)
                ins.then_inc(s_y, 1)

            def transposes(g, first=False):
                if not first:
                    pe.wait_ge(s_node_t, g)
                pe.wait_ge(s_h2, (g + 1) * G)
                for t in range(G):
                    ins = nc.tensor.transpose(tile(ps_t, t), tile(h2, t), ident[:, :])
                ins.then_inc(s_tr, 1)

            def three(dst, left, right, first=True, last=True):
                (lh, ll), (rh, rl) = left, right
                nc.tensor.matmul(dst, lh, rh, start=first, stop=False)
                nc.tensor.matmul(dst, lh, rl, start=False, stop=False)
                return nc.tensor.matmul(dst, ll, rh, start=False, stop=last)

            def nodes(g, par, more=True):
                if more:
                    pe.wait_ge(s_x1, g + 2)
                pe.wait_ge(s_h2t_lo, g + 1)
                h = (h2_hi[:, par, :], h2_lo[:, par, :])
                for t in range(G):
                    three(ps_node[:, t * K:(t + 1) * K], [tile(x, t) for x in h], (w1_hi[:, 0:K], w1_lo[:, 0:K]))
                three(ps_node_t[:, :], (w1_hi[:, :], w1_lo[:, :]), h).then_inc(s_nodeps, 1)

            def mix_products(g, par, t, first=False):
                for q in range(Q):
                    back = 1 if q < 2 else 2
                    if not (first and t < back):
                        pe.wait_ge(s_bank[q], g * G + (t + 1 - back))
                    cols = slice(q * CH, (q + 1) * CH)
                    three(mix_bank(q, t)[:, :], (tile(h2_hi[:, par, :], t), tile(h2_lo[:, par, :], t)),
                          (w2_hi[:, cols], w2_lo[:, cols])).then_inc(s_prod, 1)

            def group(g, par, first=False, more=2):
                mix_products(g, par, 0, first)
                if more > 1:
                    y_product(g + 2)
                mix_products(g, par, 1, first)
                if more > 0:
                    transposes(g + 1)
                mix_products(g, par, 2)
                if more > 0:
                    nodes(g + 1, 1 - par, more > 1)
                mix_products(g, par, 3)

            y_product(0, first=True)
            y_product(1, node_used=False)
            transposes(0, first=True)
            nodes(0, 0)
            group(0, 0, first=True)
            group(1, 1)
            with pe.Fori(1, NC // 2 - 1) as it:
                group(it * 2, 0)
                group(it * 2 + 1, 1)
            group(NC - 2, 0, more=1)
            group(NC - 1, 1, more=0)

            pe.wait_ge(s_mixed, T)
            pe.wait_ge(s_node_t, NC)

            def back(c, h, bank_used=True):
                if bank_used:
                    pe.wait_ge(s_res, c - 1)
                pe.wait_ge(s_relu, c + 1)
                for t in range(G):
                    ins = nc.tensor.transpose(tile(ps[2 + h], t), tile(act2[:, h, :], t), ident[:, :])
                ins.then_inc(s_back, 1)

            def chunk(c, h, first=False, bank_used=True):
                nc.tensor.matmul(ps[h][:, :], bs[:, :], node_t[:, bass.ds(c * CH, CH)], start=True, stop=False)
                for u in range(NU):
                    mixed = [(tile(mixed_hi, u * UJ + j), tile(mixed_lo, u * UJ + j)) for j in range(UJ)]
                    pe.wait_ge(s_hi, c * NU + (u + 1))
                    for j in range(UJ):
                        for m in mixed[j]:
                            nc.tensor.matmul(ps[h][:, :], m, adj_hi[:, u % 2, j * CH:(j + 1) * CH],
                                             start=False, stop=False)
                    pe.wait_ge(s_lo, c * NU + (u + 1))
                    for j in range(UJ):
                        ins = nc.tensor.matmul(ps[h][:, :], mixed[j][0], adj_lo[:, u % 2, j * CH:(j + 1) * CH],
                                               start=False, stop=(u == NU - 1 and j == UJ - 1))
                    ins.then_inc(s_um, 1)
                    if u == 2 and not first:
                        back(c - 1, 1 - h, bank_used)

            chunk(0, 0, first=True)
            chunk(1, 1, bank_used=False)
            chunk(2, 0, bank_used=False)
            chunk(3, 1)
            with pe.Fori(2, NC // 2) as it:
                chunk(it * 2, 0)
                chunk(it * 2 + 1, 1)
            back(NC - 1, 1)


PREP = 4 + 4 + 5 + 5 + 2


def kernel(x, adj, L0_gnn_W, L1_gnn_W1, L1_gnn_W2, L1_gnn_b):
    import numpy as np
    import concourse.bacc as bacc
    from concourse.bass_utils import run_bass_kernel_spmd

    adj = np.asarray(adj)
    arrays = {
        "x": np.ascontiguousarray(x),
        "adj": np.ascontiguousarray(adj),
        "adj_t": np.ascontiguousarray(adj.T),
        "w_t": np.ascontiguousarray(np.asarray(L0_gnn_W).T),
        "w1": np.ascontiguousarray(L1_gnn_W1),
        "w2": np.ascontiguousarray(L1_gnn_W2),
        "b": np.ascontiguousarray(L1_gnn_b),
    }
    nc = bacc.Bacc("TRN2", target_bir_lowering=False, num_devices=1)
    args = [nc.dram_tensor(n, a.shape, mybir.dt.from_np(a.dtype), kind="ExternalInput").ap() for n, a in arrays.items()]
    out = nc.dram_tensor("out", arrays["x"].shape, F32, kind="ExternalOutput").ap()
    two_graph_layers(nc, *args, out)
    result = run_bass_kernel_spmd(nc, [arrays], core_ids=[0])
    return result.results[0]["out"]
```

```python
from contextlib import ExitStack

import concourse.bass as bass
from concourse import mybir

P = 128
ALU = mybir.AluOpType
ACT = mybir.ActivationFunctionType
F32 = mybir.dt.float32
F32R = mybir.dt.float32r


class Steps:

    def __init__(self, sem, base=0):
        self.sem, self.base, self.n = sem, base, 0

    def inc(self, instruction):
        instruction.then_inc(self.sem, 1)
        self.n += 1

    def wait(self, eng):
        eng.wait_ge(self.sem, self.base + self.n)


def two_graph_layers(nc, x_in, adj, adj_t, w_t, w1, w2, b, out):
    N, F = x_in.shape
    K = w1.shape[1]
    T = N // P
    CH = 512
    NC = N // CH
    G = CH // P
    E = 3
    TR = 15
    SPLIT = (0, 2, 4, 6)
    KS = 20
    SB = 3
    RS = 4
    NS = 4
    KQ = CH // F
    Q = K // KQ
    UJ = 4
    NU = T // UJ
    EPS = 1e-5
    W2_STEP = 22
    X_LOADS = [(0, 4), (4, 16), (16, T)]
    X_LOTS = [(0, 4, 0, -1), (4, 16, 1, 1), (16, 24, 2, 13), (24, T, 2, 16)]
    X_STATS = {13: 16, 14: 20, 16: 24, 17: 28}
    assert F == P and NC == 8 and NU == 8

    with ExitStack() as ctx:
        def sb(name, shape, dtype=F32):
            return ctx.enter_context(nc.sbuf_tensor(name, shape, dtype))

        def sem(name):
            return ctx.enter_context(nc.semaphore(name))

        def alloc(stack, name, shape, dtype=F32):
            return stack.enter_context(nc.sbuf_tensor(name, shape, dtype))

        xs = sb("xs", [P, N])
        tail_sum = sb("tail_sum", [P, CH])
        near = sb("near", [P, 4, P])
        strip_sum = sb("strip_sum", [P, P])
        part_blk = sb("part_blk", [P, 2, P])
        feat = sb("feat", [P, 2, F])
        feat_hi = sb("feat_hi", [P, 2, F], F32R)
        feat_lo = sb("feat_lo", [P, 2, F], F32R)
        w_ts = sb("w_ts", [P, F])
        w1_raw = sb("w1_raw", [P, K])
        bs = sb("bs", [K, F])
        ident = sb("ident", [P, P])
        ones = sb("ones", [P, 2])
        eps = sb("eps", [P, 1])
        zero = sb("zero", [P, 1])
        stats = sb("stats", [P, T, 6])
        tmp = sb("tmp", [P, 5, T])
        ln = sb("ln", [P, T, 2])
        natsum = sb("natsum", [P, T])
        rows = sb("rows", [P, T])
        root = sb("root", [P, T])
        dnew = sb("dnew", [P, 2])
        deg = sb("deg", [P, T])
        coef = sb("coef", [P, 2, 2])
        ln2 = sb("ln2", [P, G, 2])
        w1_hi = sb("w1_hi", [P, P], F32R)
        w1_lo = sb("w1_lo", [P, P], F32R)
        w1_both = sb("w1_both", [P, 2 * K], F32R)
        PAIRS = (E + 1) * (E + 4) // 2
        far_w = (NC - 1 - E) * CH
        with ExitStack() as early:
            far0 = alloc(early, "far0", [P, far_w])
            part = alloc(early, "part", [P, N])
            held = alloc(early, "held", [P, PAIRS, G, CH])
            strips = alloc(early, "strips", [P, TR, CH])
            chunk_hi = alloc(early, "chunk_hi", [P, SB, CH], F32R)
            chunk_lo = alloc(early, "chunk_lo", [P, SB, CH], F32R)
        with ExitStack() as early:
            w2_raw = alloc(early, "w2_raw", [P, K * F])
            w2_hi = alloc(early, "w2_hi", [P, K * F], F32R)
            prods = alloc(early, "prods", [P, G, 2 * KQ * F])
            w2_lo = alloc(early, "w2_lo", [P, K * F], F32R)
        assert K * F == UJ * CH and 2 * 2 * KQ * F == UJ * CH and far_w == UJ * CH and N == 2 * far_w
        adj_hi0 = sb("adj_hi0", [P, UJ * CH], F32R)
        adj_lo0 = sb("adj_lo0", [P, UJ * CH], F32R)
        adj_lo1 = sb("adj_lo1", [P, UJ * CH], F32R)
        sb("prods_of_tiles_2_and_3", [P, UJ * CH])
        adj_hi1 = sb("adj_hi1", [P, UJ * CH], F32R)
        adj_hi, adj_lo = [adj_hi0, adj_hi1], [adj_lo0, adj_lo1]
        prop_g = sb("prop_g", [P, CH])
        prop_t = sb("prop_t", [P, N])
        node_t = prop_t[0:K, :]
        h2 = sb("h2", [P, CH])
        with ExitStack() as early:
            h2_hi = alloc(early, "h2_hi", [P, 2, CH], F32R)
        act2 = sb("act2", [P, 2, CH])
        h2_lo = sb("h2_lo", [P, 2, CH], F32R)
        node = sb("node", [P, 2, G * K])
        units = sb("units", [P, NU * UJ * CH])
        unit = [units[:, s * UJ * CH:(s + 1) * UJ * CH] for s in range(NU)]
        accs = sb("accs", [P, G, KQ * F])
        sums = sb("sums", [P, 2, CH])
        mixed_hi = sb("mixed_hi", [P, N], F32R)
        mixed_lo = sb("mixed_lo", [P, N], F32R)

        far1 = xs[:, N // 2:N]

        def far_of(k):
            n = (NC - 1 - E - k // G) * CH
            if n <= 0:
                return None
            if n == CH:
                return far0[:, (k % 2) * CH:(k % 2 + 1) * CH]
            return far1[:, 0:n] if k % 2 else far0[:, 0:n]

        FAR_TILES = (NC - 1 - E) * G

        ps = [ctx.enter_context(nc.psum_tensor(f"ps{i}", [P, CH], F32)) for i in range(8)]
        tail, psrow = ps[7], ps[7][:, 0:1]
        total = [ps[NC - 2 - c] for c in range(NC - 1)]
        ps_y, ps_node = ps[6], ps[6]
        ps_t, ps_node_t = ps[7], ps[7]

        def mix_bank(q, t):
            return ps[q + 2 * (t % 2)] if q >= 2 else ps[q]

        def scalar_banks(t):
            return [0, 1]

        s_x = [sem(f"x_landed{i}") for i in range(len(X_LOADS))]
        s_w = sem("weights_landed")
        s_far = [sem(f"far_landed{i}") for i in range(2)]
        s_near = [sem(f"near_landed{i}") for i in range(NS)]
        s_ring = [sem(f"strip_landed{i}") for i in range(RS)]
        s_unit = [sem(f"unit_landed{i}") for i in range(NU)]
        s_const = sem("constants_set")
        s_natsum = sem("natural_part_summed")
        s_part = sem("part_block_ready")
        s_added = sem("strip_added")
        s_strip_read = sem("strip_read_by_vector")
        s_tail = sem("tail_product_ready")
        s_tail_added = sem("tail_added")
        s_rowps = sem("rowsum_in_psum")
        s_rows = sem("rowsum_ready")
        s_root = sem("root_ready")
        s_coef = sem("coefficients_ready")
        s_feat = sem("features_ready")
        s_step = sem("step_multiplied")
        s_split_hi = sem("chunk_hi_ready")
        s_split_lo = sem("chunk_lo_ready")
        s_split_used = sem("split_chunk_multiplied")
        s_feat_lo = sem("features_lo_ready")
        s_done = sem("chunk_complete")
        s_v = sem("vector_steps")
        s_var = sem("variance_ready")
        s_std = sem("std_ready")
        s_evac = sem("propagated_out_of_psum_by_scalar")
        s_evacv = sem("propagated_out_of_psum_by_vector")
        s_pg = sem("propagated_group_copied")
        s_y = sem("y_ready")
        s_x1 = sem("x1_ready")
        s_passed = sem("scalar_wait_passed")
        s_var2 = sem("variance2_ready")
        s_std2 = sem("std2_ready")
        s_ln2 = sem("ln2_ready")
        s_h2 = sem("h2_ready")
        s_tr = sem("h2_transposed")
        s_h2t = sem("h2t_copied")
        s_nodeps = sem("node_in_psum")
        s_node = sem("node_copied")
        s_node_t = sem("node_t_copied")
        s_prod = sem("mix_products_ready")
        s_bank = [sem(f"mix_bank_read{q}") for q in range(Q)]
        s_pool = sem("pool_steps")
        s_sum = sem("tile_sum_ready")
        s_mixed_hi = sem("mixed_hi_ready")
        s_mixed = sem("mixed_ready")
        s_w_split = sem("weights_hi_ready")
        s_w_lo = sem("weights_lo_ready")
        s_h2t_lo = sem("h2t_lo_ready")
        s_hi = sem("unit_hi_ready")
        s_lo = sem("unit_lo_ready")
        s_pass = sem("pool_wait_passed")
        s_um = sem("unit_multiplied")
        s_relu = sem("chunk_activated")
        s_back = sem("chunk_transposed_back")
        s_res = sem("chunk_result_ready")
        s_out = sem("result_stored")

        block = ctx.enter_context(nc.Block())
        adj_u = adj_t.rearrange("(u j p) i -> u p j i", j=UJ, p=P)

        def tile(buf, t):
            return buf[:, t * P:(t + 1) * P]

        def held_slot(J, c):
            d = J - c
            assert 0 <= d <= E
            before = sum(e + 2 for e in range(d + 1, E + 1))
            return before + (c + (1 if d == E else 0)) % (d + 2)

        def moving(j):
            J = j // G
            return list(range(0, max(0, J - E))) + list(range(J + 1, NC))

        SPARE = {}
        for j, pairs in [(1, [(5, 2), (6, 3)]), (3, [(4, 2), (5, 3)]), (5, [(6, 3), (7, 4)]), (7, [(5, 3), (7, 4)])]:
            free = [held_slot(*pair) * G + i for pair in pairs for i in range(G)]
            SPARE[j] = free[:G] + free[-2:] if j == 7 else free[:NC - 1 - j // G]

        def in_ring(j):
            return 0 if j in SPARE else len(moving(j))

        def ring_slot(j, c):
            if j in SPARE:
                return SPARE[j][moving(j).index(c)]
            return (sum(in_ring(i) for i in range(j)) + moving(j).index(c)) % TR

        def place(j, slot, n=1):
            memory = held[:, :, :, :].rearrange("p a g i -> p (a g) i") if j in SPARE else strips
            return memory[:, slot:slot + n, :]

        def chunk_of(j, c):
            if c in moving(j):
                return place(j, ring_slot(j, c)).rearrange("p c i -> p (c i)")
            return held[:, held_slot(j // G, c), j % G, :]

        def block_of(j, i):
            return chunk_of(j, i // G)[:, (i % G) * P:(i % G + 1) * P]

        def ring_runs(j):
            runs = []
            for c in moving(j):
                slot = ring_slot(j, c)
                if runs and runs[-1][0] + runs[-1][2] == c and runs[-1][1] + runs[-1][2] == slot:
                    runs[-1][2] += 1
                else:
                    runs.append([c, slot, 1])
            return runs

        def strip_loads(j):
            loads = [(place(j, slot, n), c * CH, (c + n) * CH) for c, slot, n in ring_runs(j)]
            J, jj = j // G, j % G
            if jj < G - 1:
                loads.append((held[:, held_slot(J, J), jj, (jj + 1) * P:CH], (j + 1) * P, (J + 1) * CH))
            return loads

        def strip_pieces(k):
            first = k + 2
            if first // G == k // G:
                yield first * P, (k // G + 1) * CH, chunk_of(k, k // G)[:, (first % G) * P:CH]
            for c, slot, n in ring_runs(k):
                a = max(c * CH, first * P)
                if c > k // G and a < (c + n) * CH:
                    yield a, (c + n) * CH, place(k, slot, n).rearrange("p c i -> p (c i)")[:, a - c * CH:n * CH]

        def pieces_added(k):
            return sum(len(list(strip_pieces(i))) for i in range(k + 1))

        def feats(k):
            return k + 1 + max(0, k + 1 - KS)

        def near_groups(k):
            return range(k // G, min(k // G + E, NC - 1) + 1)

        def free_after(j):
            end = sum(in_ring(i) for i in range(j + 1))
            return max(i + 1 for i in range(-1, j)
                       if i < 0 or (in_ring(i) and in_ring(j) and sum(in_ring(m) for m in range(i)) < end - TR))

        def landed(loads, k, every):
            return 16 * sum(len(loads(i)) for i in range(k % every, k + 1, every))

        def at(buf, start, size):
            return buf[:, bass.ds(start, size)]

        def load_x(eng, i):
            a, b = X_LOADS[i]
            eng.dma_start(xs[:, a * F:b * F].rearrange("p (t f) -> p t f", f=F),
                          x_in[a * P:b * P, :].rearrange("(t p) f -> p t f", p=P)).then_inc(s_x[i], 16)

        @block.sync
        def _(sp):
            def load_rows(k):
                c = k // G
                if k >= NS:
                    sp.wait_ge(s_part, k - NS + 1)
                if k % G == 0 and c >= 2:
                    sp.wait_ge(s_step, (c - 1) * G)
                    sp.wait_ge(s_strip_read, (c - 1) * G)
                for J in near_groups(k):
                    first = k % G if J == c else 0
                    sp.dma_start(held[:, held_slot(J, c), first:G, (k % G) * P:(k % G + 1) * P],
                                 adj_t[(J * G + first) * P:(J + 1) * CH, k * P:(k + 1) * P].rearrange(
                                     "(j p) i -> p j i", p=P)).then_inc(s_near[k % NS], 16)
                if k < FAR_TILES:
                    if k >= 2:
                        sp.wait_ge(s_natsum, k - 1)
                    sp.dma_start(far_of(k), adj[k * P:(k + 1) * P, (c + E + 1) * CH:N]).then_inc(s_far[k % 2], 16)

            def load_strip(j):
                used = max(free_after(j), j - RS + 1)
                if used > 0:
                    sp.wait_ge(s_step, used)
                    sp.wait_ge(s_strip_read, used)
                for dst, a, b in strip_loads(j):
                    sp.dma_start(dst, adj_t[j * P:(j + 1) * P, a:b]).then_inc(s_ring[j % RS], 16)

            load_rows(0)
            load_x(sp, 0)
            load_strip(0)
            load_rows(1)
            load_x(sp, 1)
            for k in range(1, T):
                load_strip(k)
                if k + 1 < T:
                    load_rows(k + 1)

            def load_unit(c, u):
                sp.dma_start(unit[u].rearrange("p (j i) -> p j i", j=UJ),
                             adj_u[u][:, :, bass.ds(c * CH, CH)]).then_inc(s_unit[u], 16)

            sp.wait_ge(s_step, T)
            sp.wait_ge(s_strip_read, T)
            for u in range(NU):
                load_unit(0, u)
            with sp.Fori(1, NC) as c:
                for u in range(NU):
                    sp.wait_ge(s_lo, c * NU + (u + 1 - NU))
                    load_unit(c, u)
            sp.wait_ge(s_out, 16 * NC)

        @block.gpsimd
        def _(pool):
            nc.gpsimd.memset(eps[:, :], EPS).then_inc(s_const, 1)
            nc.gpsimd.memset(zero[:, :], 0.0).then_inc(s_const, 1)
            nc.gpsimd.memset(w1_hi[:, K:P].bitcast(F32), 0.0).then_inc(s_const, 1)
            nc.gpsimd.memset(w1_lo[:, K:P].bitcast(F32), 0.0).then_inc(s_const, 1)
            nc.gpsimd.memset(ones[:, :], 1.0).then_inc(s_const, 1)
            nc.gpsimd.memset(ident[:, :], 0.0).then_inc(s_const, 1)
            pool.wait_ge(s_const, 6)
            nc.gpsimd.affine_select(out=ident[:, :], in_=ident[:, :], compare_op=ALU.not_equal, fill=1.0, base=0,
                                    pattern=[[-1, P]], channel_multiplier=1).then_inc(s_const, 1)

            for k in range(KS):
                pool.wait_ge(s_ring[k % RS], landed(strip_loads, k, RS))
                if k >= 1:
                    pool.wait_ge(s_added, pieces_added(k - 1))
                for a, b, src in strip_pieces(k):
                    if k == 0:
                        nc.gpsimd.tensor_copy(part[:, a:b], src).then_inc(s_added, 1)
                    else:
                        nc.gpsimd.tensor_tensor(part[:, a:b], part[:, a:b], src, ALU.add).then_inc(s_added, 1)

            def split_low(k, q):
                n = (k - KS) * len(SPLIT) + q
                pool.wait_ge(s_split_hi, n + 1)
                nc.gpsimd.tensor_tensor(chunk_lo[:, n % SB, :], chunk_of(k, SPLIT[q]),
                                        chunk_hi[:, n % SB, :].bitcast(F32), ALU.subtract).then_inc(s_split_lo, 1)

            for k in range(KS, T):
                split_low(k, 0)
                pool.wait_ge(s_feat, feats(k))
                nc.gpsimd.tensor_tensor(feat_lo[:, k % 2, :], feat[:, k % 2, :], feat_hi[:, k % 2, :].bitcast(F32),
                                        ALU.subtract).then_inc(s_feat_lo, 1)
                for q in range(1, len(SPLIT)):
                    split_low(k, q)

            def merge(g, par, t, step):
                idx = g * G + t
                p, a = prods[:, t, :], accs[:, t, :]
                pool.wait_ge(s_bank[Q - 1], idx + 1)
                if len(scalar_banks(t)) > 1:
                    pool.wait_ge(s_bank[1], idx + 1)
                    step.inc(nc.gpsimd.tensor_tensor(a, a, p[:, CH:2 * CH], ALU.add))
                    step.wait(pool)
                step.inc(nc.gpsimd.tensor_tensor(a[:, 0:2 * F], a[:, 0:2 * F], a[:, 2 * F:4 * F], ALU.add))
                step.wait(pool)
                nc.gpsimd.tensor_tensor(tile(sums[:, par, :], t), a[:, 0:F], a[:, F:2 * F],
                                        ALU.add).then_inc(s_sum, 1)

            def low_part(g, par):
                pool.wait_ge(s_mixed_hi, g + 1)
                pool.sem_inc(s_pass, 1)
                dst = bass.ds(g * CH, CH)
                nc.gpsimd.tensor_tensor(mixed_lo[:, dst], sums[:, par, :], mixed_hi[:, dst].bitcast(F32),
                                        ALU.subtract).then_inc(s_mixed, 1)

            def group(g, par, step, low_before=True, sums_used=True):
                for t in range(G):
                    if t == 0 and sums_used:
                        pool.wait_ge(s_mixed, g - 1)
                    merge(g, par, t, step)
                    if t == 2 and low_before:
                        low_part(g - 1, 1 - par)

            per = 2 * sum(len(scalar_banks(t)) for t in range(G))
            step = Steps(s_pool)
            group(0, 0, step, low_before=False, sums_used=False)
            group(1, 1, step, sums_used=False)
            with pool.Fori(1, NC // 2) as it:
                step = Steps(s_pool, it * per)
                group(it * 2, 0, step)
                group(it * 2 + 1, 1, step)
                assert step.n == per
            low_part(NC - 1, 1)

        @block.scalar
        def _(act):
            act.dma_start(w_ts[:, :], w_t).then_inc(s_w, 16)
            act.dma_start(w1_raw[:, :], w1).then_inc(s_w, 16)
            act.dma_start(bs[:, :], b).then_inc(s_w, 16)
            act.wait_ge(s_const, 7)

            def sum_rows(k):
                act.wait_ge(s_far[k % 2], 16 * (k // 2 + 1))
                nc.scalar.activation(far_of(k), far_of(k), ACT.Copy,
                                     accum_out=natsum[:, k:k + 1]).then_inc(s_natsum, 1)

            def std_x(lot):
                n = X_LOTS[lot][1] - X_LOTS[lot][0]
                act.wait_ge(s_var, lot + 1)
                nc.scalar.activation(tmp[:, 0, 0:n], tmp[:, 4, 0:n], ACT.Sqrt, bias=zero[:, 0:1]).then_inc(s_std, 1)

            def split_high(k, q):
                n = (k - KS) * len(SPLIT) + q
                if n >= SB:
                    step, q_before = divmod(n - SB, len(SPLIT))
                    step += KS
                    if q_before == len(SPLIT) - 1:
                        act.wait_ge(s_step, step + 1)
                    elif step == T - 1:
                        act.wait_ge(s_done, SPLIT[q_before] + 1)
                    else:
                        act.wait_ge(s_split_used, (step - KS) * (len(SPLIT) - 1) + q_before + 1)
                act.wait_ge(s_part, k + 1)
                act.wait_ge(s_ring[k % RS], landed(strip_loads, k, RS))
                nc.scalar.activation(chunk_hi[:, n % SB, :], chunk_of(k, SPLIT[q]), ACT.Copy).then_inc(s_split_hi, 1)

            std_x(0)
            sum_rows(0)
            for k in range(T):
                act.wait_ge(s_rows, k + 1)
                nc.scalar.activation(root[:, k:k + 1], rows[:, k:k + 1], ACT.Sqrt,
                                     bias=zero[:, 0:1]).then_inc(s_root, 1)
                if k >= KS:
                    split_high(k, 0)
                act.wait_ge(s_coef, k + 1)
                if k >= 2:
                    act.wait_ge(s_step, k - 1)
                for dst in (feat, feat_hi) if k >= KS else (feat,):
                    nc.scalar.activation(dst[:, k % 2, :], tile(xs, k), ACT.Relu, scale=coef[:, k % 2, 0:1],
                                         bias=coef[:, k % 2, 1:2]).then_inc(s_feat, 1)
                for lot, (_, _, _, step) in enumerate(X_LOTS):
                    if k == step + 2 and lot > 0:
                        std_x(lot)
                if k + 1 < FAR_TILES:
                    sum_rows(k + 1)
                if k + 2 == FAR_TILES - G:
                    act.wait_ge(s_natsum, FAR_TILES - G)
                    load_x(act, 2)
                for q in range(1, len(SPLIT)):
                    if k >= KS:
                        split_high(k, q)
                if k == FAR_TILES + 1:
                    act.wait_ge(s_natsum, FAR_TILES)
                    act.dma_start(w2_raw[:, :].rearrange("c (k f) -> c k f", f=F),
                                  w2.rearrange("k c f -> c k f")).then_inc(s_w, 16)
                if W2_STEP <= k < W2_STEP + Q:
                    cols = slice((k - W2_STEP) * CH, (k - W2_STEP + 1) * CH)
                    act.wait_ge(s_w, 64)
                    nc.scalar.activation(w2_hi[:, cols], w2_raw[:, cols], ACT.Copy).then_inc(s_w_split, 1)
                    if k == W2_STEP:
                        for dst in (w1_hi, w1_both):
                            nc.scalar.activation(dst[:, 0:K], w1_raw[:, :], ACT.Copy).then_inc(s_w_split, 1)

            act.wait_ge(s_done, 1)
            nc.scalar.activation(prop_g[:, :], total[0][:, :], ACT.Copy).then_inc(s_pg, 1)

            def leave_psum(c):
                if c < NC - 2:
                    act.wait_ge(s_done, c + 1)
                else:
                    act.wait_ge(s_step, T)
                nc.scalar.activation(prop_t[:, c * CH:(c + 1) * CH], total[c][:, :], ACT.Copy).then_inc(s_evac, 1)

            def pass_wait(semaphore, value):
                act.wait_ge(semaphore, value)
                act.sem_inc(s_passed, 1)

            def copy_group(g):
                pass_wait(s_y, g)
                nc.scalar.activation(prop_g[:, :], at(prop_t, g * CH, CH), ACT.Copy).then_inc(s_pg, 1)

            def std(g):
                act.wait_ge(s_var2, g + 1)
                nc.scalar.activation(tmp[:, 0, 0:G], tmp[:, 4, 0:G], ACT.Sqrt, bias=zero[:, 0:1]).then_inc(s_std2, 1)

            def normed(g, first=False):
                if not first:
                    act.wait_ge(s_tr, g)
                pass_wait(s_ln2, g + 1)
                for t in range(G):
                    nc.scalar.activation(tile(h2, t), at(xs, g * CH + t * P, P), ACT.Relu, scale=ln2[:, t, 0:1],
                                         bias=ln2[:, t, 1:2]).then_inc(s_h2, 1)

            def high_part(g, par, slot_used=True):
                act.wait_ge(s_tr, g + 1)
                if slot_used:
                    act.wait_ge(s_prod, (g - 1) * (Q * G))
                nc.scalar.activation(h2_hi[:, par, :], ps_t[:, :], ACT.Copy).then_inc(s_h2t, 1)

            def copy_node_t(g):
                pass_wait(s_nodeps, g + 1)
                nc.scalar.activation(node_t[:, bass.ds(g * CH, CH)], ps_node_t[0:K, :], ACT.Copy).then_inc(s_node_t, 1)

            def products(g, par, t, first=False):
                idx = g * G + t
                if not first:
                    act.wait_ge(s_sum, idx - G + 1)
                act.wait_ge(s_node, g + 1)
                for q in scalar_banks(t):
                    act.wait_ge(s_prod, g * (Q * G) + (t * Q + q + 1))
                    for kk in range(KQ):
                        k = q * KQ + kk
                        ins = nc.scalar.activation(prods[:, t, k * F:(k + 1) * F], mix_bank(q, t)[:, kk * F:(kk + 1) * F],
                                                   ACT.Copy, scale=node[:, par, t * K + k:t * K + k + 1])
                    ins.then_inc(s_bank[q], 1)

            def mixed_high(g, par):
                pass_wait(s_sum, (g + 1) * G)
                nc.scalar.activation(mixed_hi[:, bass.ds(g * CH, CH)], sums[:, par, :],
                                     ACT.Copy).then_inc(s_mixed_hi, 1)

            def group(g, par, first=False, more=2, slot_used=True):
                if more > 1:
                    copy_group(g + 2)
                products(g, par, 0, first)
                if more > 0:
                    normed(g + 1)
                products(g, par, 1, first)
                if more > 0:
                    high_part(g + 1, 1 - par, slot_used)
                products(g, par, 2, first)
                if not first:
                    mixed_high(g - 1, 1 - par)
                if more > 1:
                    std(g + 2)
                products(g, par, 3, first)
                if more > 0:
                    copy_node_t(g + 1)

            leave_psum(2)
            act.wait_ge(s_done, 2)
            act.wait_ge(s_y, 1)
            nc.scalar.activation(prop_g[:, :], total[1][:, :], ACT.Copy).then_inc(s_pg, 1)
            leave_psum(4)
            std(0)
            leave_psum(6)
            normed(0, first=True)
            high_part(0, 0, slot_used=False)
            std(1)
            copy_node_t(0)
            act.wait_ge(s_evac, 3)
            act.wait_ge(s_evacv, 3)
            group(0, 0, first=True, slot_used=False)
            group(1, 1)
            with act.Fori(1, NC // 2 - 1) as it:
                group(it * 2, 0)
                group(it * 2 + 1, 1)
            group(NC - 2, 0, more=1)
            group(NC - 1, 1, more=0)

            def activate(c, h):
                act.wait_ge(s_um, c * NU + NU)
                nc.scalar.activation(act2[:, h, :], ps[h][:, :], ACT.Relu).then_inc(s_relu, 1)

            def store(c):
                act.wait_ge(s_res, c + 1)
                act.dma_start(out.rearrange("(t p) f -> p t f", p=P)[:, bass.ds(c * G, G), :],
                              at(xs, c * CH, CH).rearrange("p (t f) -> p t f", f=F)).then_inc(s_out, 16)

            def chunk(c, h, first=False):
                for u in range(NU):
                    if not (first and u < 2):
                        act.wait_ge(s_um, c * NU + (u - 1))
                    if first and u == 1:
                        act.wait_ge(s_prod, Q * T)
                    act.wait_ge(s_unit[u], c * 16 + 16)
                    nc.scalar.activation(adj_hi[u % 2][:, :], unit[u], ACT.Copy).then_inc(s_hi, 1)
                    if first and u == 1:
                        mixed_high(NC - 1, 1)
                    if u == 1 and not first:
                        activate(c - 1, 1 - h)
                    if u == 5 and not first:
                        store(c - 1)

            chunk(0, 0, first=True)
            chunk(1, 1)
            with act.Fori(1, NC // 2) as it:
                chunk(it * 2, 0)
                chunk(it * 2 + 1, 1)
            activate(NC - 1, 1)
            store(NC - 1)

        @block.vector
        def _(dve):
            v = Steps(s_v)

            def then(instruction, step):
                step.inc(instruction)
                step.wait(dve)

            def variance(st, n, step):
                total, gap, sq, var = tmp[:, 1, 0:n], tmp[:, 2, 0:n], tmp[:, 3, 0:n], tmp[:, 4, 0:n]
                step.inc(nc.vector.tensor_tensor(total, st[:, 0:n, 1], st[:, 0:n, 4], ALU.add))
                step.inc(nc.vector.tensor_tensor(gap, st[:, 0:n, 1], st[:, 0:n, 4], ALU.subtract))
                then(nc.vector.tensor_tensor(sq, st[:, 0:n, 2], st[:, 0:n, 5], ALU.add), step)
                then(nc.vector.tensor_scalar(sq, sq, 1.0 / F, EPS, ALU.mult, ALU.add), step)
                then(nc.vector.tensor_tensor(gap, gap, gap, ALU.mult), step)
                return nc.vector.scalar_tensor_tensor(out=var, in0=gap, scalar=0.25, in1=sq, op0=ALU.mult, op1=ALU.add)

            def inverse_root(square, rt, dst, s, step):
                then(nc.vector.reciprocal(dst, rt), step)
                then(nc.vector.tensor_tensor(s, dst, dst, ALU.mult), step)
                then(nc.vector.tensor_tensor(s, s, square, ALU.mult), step)
                then(nc.vector.tensor_scalar(s, s, -0.5, 1.5, ALU.mult, ALU.add), step)
                then(nc.vector.tensor_tensor(dst, dst, s, ALU.mult), step)

            def ln_scales(n, dst, step):
                inverse_root(tmp[:, 4, 0:n], tmp[:, 0, 0:n], tmp[:, 2, 0:n], tmp[:, 3, 0:n], step)
                rstd = tmp[:, 2, 0:n]
                step.inc(nc.vector.tensor_copy(dst[:, 0:n, 0], rstd))
                return nc.vector.scalar_tensor_tensor(out=dst[:, 0:n, 1], in0=tmp[:, 1, 0:n], scalar=-0.5, in1=rstd,
                                                      op0=ALU.mult, op1=ALU.mult)

            def stats_x(load, a, b):
                dve.wait_ge(s_x[load], 16)
                for t in range(a, b):
                    v.inc(nc.vector.bn_stats(stats[:, t, :], tile(xs, t)))

            def var_x(lot):
                a, b, load, _ = X_LOTS[lot]
                if a not in X_STATS.values():
                    stats_x(load, a, b)
                v.wait(dve)
                variance(stats[:, a:b, :], b - a, v).then_inc(s_var, 1)

            def scales_x(lot):
                a, b, _, _ = X_LOTS[lot]
                dve.wait_ge(s_std, lot + 1)
                then(ln_scales(b - a, ln[:, a:b, :], v), v)

            def add_strip(k):
                for a, b, src in strip_pieces(k):
                    v.inc(nc.vector.tensor_tensor(part[:, a:b], part[:, a:b], src, ALU.add))
                    yield

            def near_sum(k, pieces):
                c, jj = k // G, k % G
                cols = slice(jj * P, (jj + 1) * P)
                dve.wait_ge(s_near[k % NS], landed(near_groups, k, NS))
                own, *others = [held[:, held_slot(J, c), :, cols] for J in near_groups(k)]

                def add(dst, a, b, read_next=True):
                    v.inc(nc.vector.tensor_tensor(dst, a, b, ALU.add))
                    n = v.n
                    next(pieces, None)
                    if read_next:
                        dve.wait_ge(v.sem, n)

                if len(others) <= 1:
                    if others:
                        v.inc(nc.vector.tensor_tensor(near[:, jj:G, :], own[:, jj:G, :], others[0][:, jj:G, :], ALU.add))
                    else:
                        v.inc(nc.vector.tensor_copy(near[:, jj:G, :], own[:, jj:G, :]))
                    if jj > 0 and others:
                        v.inc(nc.vector.tensor_copy(near[:, 0:jj, :], others[0][:, 0:jj, :]))
                    elif jj > 0:
                        v.inc(nc.vector.memset(near[:, 0:jj, :], 0.0))
                    for _ in pieces:
                        pass
                    v.wait(dve)
                else:
                    add(near[:, :, :], others[0], others[1])
                    for other in others[2:]:
                        add(near[:, :, :], near[:, :, :], other)
                    add(near[:, jj:G, :], near[:, jj:G, :], own[:, jj:G, :])
                    for _ in pieces:
                        pass
                add(near[:, 0:2, :], near[:, 0:2, :], near[:, 2:4, :], read_next=False)
                v.wait(dve)
                if k >= 2:
                    dve.wait_ge(s_added, pieces_added(min(k - 2, KS - 1)))
                    add(strip_sum[:, :], block_of(k - 1, k), tile(part, k))
                if k == 0:
                    return nc.vector.tensor_tensor(part_blk[:, 0, :], near[:, 0, :], near[:, 1, :], ALU.add)
                add(near[:, 1, :], near[:, 1, :], block_of(0, 1) if k == 1 else strip_sum[:, :])
                if k >= 2:
                    dve.wait_ge(s_rowps, k - 1)
                return nc.vector.tensor_tensor(part_blk[:, k % 2, :], near[:, 0, :], near[:, 1, :], ALU.add)

            def degree(k):
                if k in X_STATS:
                    stats_x(2, X_STATS[k], X_STATS[k] + 2)
                dve.wait_ge(s_rowps, k + 1)
                if k < FAR_TILES:
                    dve.wait_ge(s_natsum, k + 1)
                    nc.vector.tensor_tensor(rows[:, k:k + 1], psrow, natsum[:, k:k + 1], ALU.add).then_inc(s_rows, 1)
                else:
                    nc.vector.tensor_copy(rows[:, k:k + 1], psrow).then_inc(s_rows, 1)
                if k in X_STATS:
                    stats_x(2, X_STATS[k] + 2, X_STATS[k] + 4)
                dve.wait_ge(s_root, k + 1)
                inverse_root(rows[:, k:k + 1], root[:, k:k + 1], deg[:, k:k + 1], dnew[:, 0:1], v)
                if k >= 2:
                    dve.wait_ge(s_feat, feats(k - 2))
                nc.vector.tensor_scalar(coef[:, k % 2, :], ln[:, k, :], deg[:, k:k + 1], None,
                                        ALU.mult).then_inc(s_coef, 1)

            near_sum(0, iter(())).then_inc(s_part, 1)
            var_x(0)
            scales_x(0)
            degree(0)
            dve.wait_ge(s_ring[0], landed(strip_loads, 0, RS))
            near_sum(1, iter(())).then_inc(s_part, 1)
            for k in range(T):
                dve.wait_ge(s_tail, k + 1)
                if k == 0:
                    nc.vector.tensor_copy(tail_sum[:, :], tail[:, :]).then_inc(s_tail_added, 1)
                else:
                    dve.wait_ge(s_tail_added, k)
                    nc.vector.tensor_tensor(tail_sum[:, :], tail_sum[:, :], tail[:, :], ALU.add)\
                        .then_inc(s_tail_added, 1)
                if k + 1 < T:
                    degree(k + 1)
                if k + 2 < T:
                    dve.wait_ge(s_ring[(k + 1) % RS], landed(strip_loads, k + 1, RS))
                    near_sum(k + 2, add_strip(k) if k >= KS else iter(())).then_inc(s_part, 1)
                v.wait(dve)
                dve.wait_ge(s_part, min(k + 3, T))
                dve.sem_inc(s_strip_read, 1)
                for lot, (_, _, _, step) in enumerate(X_LOTS):
                    if k == step:
                        var_x(lot)
                    if k == step + 1 and lot > 0:
                        scales_x(lot)
                if W2_STEP + Q <= k < W2_STEP + 2 * Q:
                    cols = slice((k - W2_STEP - Q) * CH, (k - W2_STEP - Q + 1) * CH)
                    dve.wait_ge(s_w_split, Q + 2)
                    nc.vector.tensor_tensor(w2_lo[:, cols], w2_raw[:, cols], w2_hi[:, cols].bitcast(F32),
                                            ALU.subtract).then_inc(s_w_lo, 1)
                    if k == W2_STEP + Q:
                        for dst in (w1_lo[:, 0:K], w1_both[:, K:2 * K]):
                            nc.vector.tensor_tensor(dst, w1_raw[:, :], w1_hi[:, 0:K].bitcast(F32),
                                                    ALU.subtract).then_inc(s_w_lo, 1)

            def leave_psum(c):
                dve.wait_ge(s_done, c + 1)
                nc.vector.tensor_copy(prop_t[:, c * CH:(c + 1) * CH], total[c][:, :]).then_inc(s_evacv, 1)


            def prep_x1(g, step):
                dve.wait_ge(s_y, g + 1)
                for t in range(G):
                    xt = at(xs, g * CH + t * P, P)
                    step.inc(nc.vector.scalar_tensor_tensor(out=xt, in0=tile(ps_y, t), scalar=at(deg, g * G + t, 1),
                                                            in1=xt, op0=ALU.mult, op1=ALU.add))
                step.wait(dve)
                dve.sem_inc(s_x1, 1)

            def prep_var(g, step):
                for t in range(G):
                    step.inc(nc.vector.bn_stats(stats[:, t, :], at(xs, g * CH + t * P, P)))
                step.wait(dve)
                variance(stats, G, step).then_inc(s_var2, 1)

            def prep_ln(g, step):
                dve.wait_ge(s_std2, g + 1)
                then(ln_scales(G, ln2, step), step)
                dve.sem_inc(s_ln2, 1)

            def prep_lo(g, par):
                dve.wait_ge(s_h2t, g + 1)
                nc.vector.tensor_tensor(h2_lo[:, par, :], ps_t[:, :], h2_hi[:, par, :].bitcast(F32),
                                        ALU.subtract).then_inc(s_h2t_lo, 1)

            def copy_node(g, par):
                dve.wait_ge(s_nodeps, g + 1)
                nc.vector.tensor_reduce(
                    out=node[:, par, :].rearrange("p (t k) -> p t k", t=G),
                    in_=ps_node[:, 0:G * 2 * K].rearrange("p (t h k) -> p t k h", t=G, h=2),
                    axis=mybir.AxisListType.X, op=ALU.add).then_inc(s_node, 1)

            def combine(g, par, t, step, first=False):
                idx = g * G + t
                if not first:
                    dve.wait_ge(s_sum, idx - G + 1)
                dve.wait_ge(s_node, g + 1)
                dve.wait_ge(s_bank[0], idx + 1)
                mine = [q for q in range(Q) if q not in scalar_banks(t)]
                for q in mine:
                    dve.wait_ge(s_prod, g * (Q * G) + (t * Q + q + 1))
                    for kk in range(KQ):
                        k = q * KQ + kk
                        acc = accs[:, t, kk * F:(kk + 1) * F]
                        before = acc
                        if q == mine[0]:
                            before = prods[:, t, kk * F:(kk + 1) * F]
                        elif kk < KQ - 1:
                            dve.wait_ge(step.sem, step.base + (step.n - KQ + 2))
                        else:
                            dve.wait_ge(s_bank[q - 1], idx + 1)
                        ins = nc.vector.scalar_tensor_tensor(out=acc, in0=mix_bank(q, t)[:, kk * F:(kk + 1) * F],
                                                             scalar=node[:, par, t * K + k:t * K + k + 1],
                                                             in1=before, op0=ALU.mult, op1=ALU.add)
                        if kk < KQ - 1:
                            step.inc(ins)
                        else:
                            ins.then_inc(s_bank[q], 1)

            def group(g, par, step, first=False, more=2):
                combine(g, par, 0, step, first)
                if more > 1:
                    prep_x1(g + 2, step)
                combine(g, par, 1, step, first)
                if more > 0:
                    prep_lo(g + 1, 1 - par)
                if more > 1:
                    prep_var(g + 2, step)
                combine(g, par, 2, step, first)
                if more > 0:
                    copy_node(g + 1, 1 - par)
                if more > 1:
                    prep_ln(g + 2, step)
                combine(g, par, 3, step, first)

            prep_x1(0, v)
            prep_var(0, v)
            leave_psum(3)
            prep_ln(0, v)
            leave_psum(5)
            dve.wait_ge(s_tail_added, T)
            nc.vector.tensor_copy(prop_t[:, N - CH:N], tail_sum[:, :]).then_inc(s_evacv, 1)
            prep_x1(1, v)
            prep_lo(0, 0)
            prep_var(1, v)
            prep_ln(1, v)
            copy_node(0, 0)
            group(0, 0, v, first=True)
            per = 2 * ((KQ - 1) * sum(Q - len(scalar_banks(t)) for t in range(G)) + PREP)
            group(1, 1, v)
            base = v.n - per
            with dve.Fori(1, NC // 2 - 1) as it:
                step = Steps(s_v, it * per + base)
                group(it * 2, 0, step)
                group(it * 2 + 1, 1, step)
                assert step.n == per, (step.n, per)
            step = Steps(s_v, base + per * (NC // 2 - 1))
            group(NC - 2, 0, step, more=1)
            group(NC - 1, 1, step, more=0)

            def add_back(c, h):
                dve.wait_ge(s_back, c + 1)
                nc.vector.tensor_tensor(at(xs, c * CH, CH), ps[2 + h][:, :], at(xs, c * CH, CH),
                                        ALU.add).then_inc(s_res, 1)

            def chunk(c, h, first=False):
                for u in range(NU):
                    if first and u == 0:
                        dve.wait_ge(s_prod, Q * T)
                    if first and u == 1:
                        dve.wait_ge(s_sum, T - G + 2)
                    dve.wait_ge(s_hi, c * NU + (u + 1))
                    nc.vector.tensor_tensor(adj_lo[u % 2][:, :], unit[u], adj_hi[u % 2][:, :].bitcast(F32),
                                            ALU.subtract).then_inc(s_lo, 1)
                    if u == 3 and not first:
                        add_back(c - 1, 1 - h)

            chunk(0, 0, first=True)
            chunk(1, 1)
            with dve.Fori(1, NC // 2) as it:
                chunk(it * 2, 0)
                chunk(it * 2 + 1, 1)
            add_back(NC - 1, 1)

        @block.tensor
        def _(pe):
            pe.wait_ge(s_const, 7)

            def row_sum(k, slot):
                pe.wait_ge(s_part, k + 1)
                nc.tensor.matmul(psrow, part_blk[:, slot, :], ones[:, 0:1], start=True, stop=True)\
                    .then_inc(s_rowps, 1)

            def y_product(g, first=False, node_used=True):
                if not first:
                    pe.wait_ge(s_x1, g)
                    if node_used:
                        pe.wait_ge(s_node, g - 1)
                pe.wait_ge(s_pg, g + 1)
                for t in range(G):
                    ins = nc.tensor.matmul(tile(ps_y, t), tile(prop_g, t), w_ts[:, :], start=True, stop=True)
                ins.then_inc(s_y, 1)

            def three(dst, left, right, first=True, last=True):
                (lh, ll), (rh, rl) = left, right
                nc.tensor.matmul(dst, lh, rh, start=first, stop=False)
                nc.tensor.matmul(dst, lh, rl, start=False, stop=False)
                return nc.tensor.matmul(dst, ll, rh, start=False, stop=last)

            def step1(k):
                first, last = k == 0, k == T - 1
                whole = feat[:, k % 2, :]
                parts = feat_hi[:, k % 2, :], feat_lo[:, k % 2, :]
                pe.wait_ge(s_ring[k % RS], landed(strip_loads, k, RS))
                pe.wait_ge(s_feat, feats(k - 1) + 1)
                nc.tensor.matmul(tail[:, :], whole, chunk_of(k, NC - 1), start=True, stop=True).then_inc(s_tail, 1)
                for c in range(NC - 1):
                    if c == 2 and not last:
                        pe.wait_ge(s_tail_added, k + 1)
                        row_sum(k + 1, (k + 1) % 2)
                    if k >= KS and c in SPLIT:
                        q = SPLIT.index(c)
                        n = (k - KS) * len(SPLIT) + q
                        pe.wait_ge(s_feat_lo, k - KS + 1)
                        pe.wait_ge(s_split_lo, n + 1)
                        ins = three(total[c][:, :], parts, (chunk_hi[:, n % SB, :], chunk_lo[:, n % SB, :]), first, last)
                        if q < len(SPLIT) - 1 and not last:
                            ins.then_inc(s_split_used, 1)
                    else:
                        ins = nc.tensor.matmul(total[c][:, :], whole, chunk_of(k, c), start=first, stop=last)
                    if last:
                        if c < NC - 2:
                            ins.then_inc(s_done, 1)
                        if c == 2:
                            y_product(0, first=True)
                ins.then_inc(s_step, 1)

            row_sum(0, 0)
            for k in range(T):
                step1(k)
            pe.wait_ge(s_w_lo, Q + 2)


            def transposes(g, first=False):
                if not first:
                    pe.wait_ge(s_node_t, g)
                pe.wait_ge(s_h2, (g + 1) * G)
                for t in range(G):
                    ins = nc.tensor.transpose(tile(ps_t, t), tile(h2, t), ident[:, :])
                ins.then_inc(s_tr, 1)

            def nodes(g, par, more=True):
                if more:
                    pe.wait_ge(s_x1, g + 2)
                pe.wait_ge(s_h2t_lo, g + 1)
                h = (h2_hi[:, par, :], h2_lo[:, par, :])
                for t in range(G):
                    dst = ps_node[:, t * 2 * K:(t + 1) * 2 * K]
                    nc.tensor.matmul(dst, tile(h[0], t), w1_both[:, :], start=True, stop=False)
                    nc.tensor.matmul(dst, tile(h[1], t), w1_both[:, :], start=False, stop=True)
                three(ps_node_t[:, :], (w1_hi[:, :], w1_lo[:, :]), h).then_inc(s_nodeps, 1)

            def mix_products(g, par, t, first=False):
                for q in range(Q):
                    if first and t == 0 and q == 0:
                        pe.wait_ge(s_evac, 3)
                        pe.wait_ge(s_evacv, 3)
                    back = 1 if q < 2 else 2
                    if not (first and t < back):
                        pe.wait_ge(s_bank[q], g * G + (t + 1 - back))
                    cols = slice(q * CH, (q + 1) * CH)
                    three(mix_bank(q, t)[:, :], (tile(h2_hi[:, par, :], t), tile(h2_lo[:, par, :], t)),
                          (w2_hi[:, cols], w2_lo[:, cols])).then_inc(s_prod, 1)

            def group(g, par, first=False, more=2):
                mix_products(g, par, 0, first)
                if more > 1:
                    y_product(g + 2)
                mix_products(g, par, 1, first)
                if more > 0:
                    transposes(g + 1)
                mix_products(g, par, 2)
                if more > 0:
                    nodes(g + 1, 1 - par, more > 1)
                mix_products(g, par, 3)

            y_product(1, node_used=False)
            transposes(0, first=True)
            nodes(0, 0)
            group(0, 0, first=True)
            group(1, 1)
            with pe.Fori(1, NC // 2 - 1) as it:
                group(it * 2, 0)
                group(it * 2 + 1, 1)
            group(NC - 2, 0, more=1)
            group(NC - 1, 1, more=0)

            pe.wait_ge(s_node_t, NC)

            def back(c, h, bank_used=True):
                if bank_used:
                    pe.wait_ge(s_res, c - 1)
                pe.wait_ge(s_relu, c + 1)
                for t in range(G):
                    ins = nc.tensor.transpose(tile(ps[2 + h], t), tile(act2[:, h, :], t), ident[:, :])
                ins.then_inc(s_back, 1)

            def chunk(c, h, first=False, bank_used=True, bank_left=None):
                if bank_left is not None:
                    pe.wait_ge(bank_left, T)
                nc.tensor.matmul(ps[h][:, :], bs[:, :], node_t[:, bass.ds(c * CH, CH)], start=True, stop=False)
                for u in range(NU):
                    mixed = [(tile(mixed_hi, u * UJ + j), tile(mixed_lo, u * UJ + j)) for j in range(UJ)]
                    pe.wait_ge(s_hi, c * NU + (u + 1))
                    if first:
                        pe.wait_ge(s_mixed, u + 1)
                    for j in range(UJ):
                        for m in mixed[j]:
                            nc.tensor.matmul(ps[h][:, :], m, adj_hi[u % 2][:, j * CH:(j + 1) * CH],
                                             start=False, stop=False)
                    pe.wait_ge(s_lo, c * NU + (u + 1))
                    for j in range(UJ):
                        ins = nc.tensor.matmul(ps[h][:, :], mixed[j][0], adj_lo[u % 2][:, j * CH:(j + 1) * CH],
                                               start=False, stop=(u == NU - 1 and j == UJ - 1))
                    ins.then_inc(s_um, 1)
                    if u == 2 and not first:
                        back(c - 1, 1 - h, bank_used)

            chunk(0, 0, first=True, bank_left=s_bank[0])
            chunk(1, 1, bank_used=False, bank_left=s_bank[1])
            chunk(2, 0, bank_used=False)
            chunk(3, 1)
            with pe.Fori(2, NC // 2) as it:
                chunk(it * 2, 0)
                chunk(it * 2 + 1, 1)
            back(NC - 1, 1)


PREP = 4 + 4 + 5 + 5 + 2


def kernel(x, adj, L0_gnn_W, L1_gnn_W1, L1_gnn_W2, L1_gnn_b):
    import numpy as np
    import concourse.bacc as bacc
    from concourse.bass_utils import run_bass_kernel_spmd

    adj = np.asarray(adj)
    arrays = {
        "x": np.ascontiguousarray(x),
        "adj": np.ascontiguousarray(adj),
        "adj_t": np.ascontiguousarray(adj.T),
        "w_t": np.ascontiguousarray(np.asarray(L0_gnn_W).T),
        "w1": np.ascontiguousarray(L1_gnn_W1),
        "w2": np.ascontiguousarray(L1_gnn_W2),
        "b": np.ascontiguousarray(L1_gnn_b),
    }
    nc = bacc.Bacc("TRN2", target_bir_lowering=False, num_devices=1)
    args = [nc.dram_tensor(n, a.shape, mybir.dt.from_np(a.dtype), kind="ExternalInput").ap() for n, a in arrays.items()]
    out = nc.dram_tensor("out", arrays["x"].shape, F32, kind="ExternalOutput").ap()
    two_graph_layers(nc, *args, out)
    result = run_bass_kernel_spmd(nc, [arrays], core_ids=[0])
    return result.results[0]["out"]
```
